# Optimizing a Trainium2 kernel written in Bass

```python
import numpy as np
import jax
import jax.numpy as jnp

def _softmax(x, axis=-1):
    return jax.nn.softmax(x, axis=axis)

def _gelu(x):
    return jax.nn.gelu(x, approximate=True)

def _silu(x):
    return jax.nn.silu(x)

def _sigmoid(x):
    return jax.nn.sigmoid(x)

def _layernorm(x, axis=-1, eps=1e-05):
    m = jnp.mean(x, axis=axis, keepdims=True)
    v = jnp.var(x, axis=axis, keepdims=True)
    return (x - m) / jnp.sqrt(v + eps)

def _scatter_add(tgt, idx, src, axis=0):
    return tgt.at[idx].add(src)

def _segment_sum(src, seg, n):
    return jax.ops.segment_sum(src, seg, n)
kernel_name = 'mk_cond_resid_d4_seqx_r8_8ac655'

def setup_inputs(seed: int=0):
    np.random.seed(seed)
    _w = jnp.asarray

    def _rec_inputs():
        import jax
        import jax.numpy as jnp
        _rk = jax.random.key(seed)
        x = 7.22e-05 + 1 * jax.random.normal(jax.random.fold_in(_rk, 1), (8, 128, 512), jnp.float32)
        _lenS = 128 - jax.random.randint(jax.random.fold_in(_rk, 7), (8,), 0, max(1, 128 // 4) + 1, jnp.int32)
        _lenS2 = 128 - jax.random.randint(jax.random.fold_in(_rk, 8), (8,), 0, max(1, 128 // 4) + 1, jnp.int32)
        condB_coeff = 0.00219231 + 0.0100837 * jax.random.normal(jax.random.fold_in(_rk, 11), (8,), jnp.float32)
        itok_B_0_2 = jax.random.randint(jax.random.fold_in(_rk, 13), (8,), 0, 3, jnp.int32)
        itok_B_14_62 = jax.random.randint(jax.random.fold_in(_rk, 14), (8,), 14, 63, jnp.int32)
        itok_B_3_7 = jax.random.randint(jax.random.fold_in(_rk, 15), (8,), 3, 8, jnp.int32)
        _validS = jnp.arange(128)[None, :] < _lenS[:, None]
        _validS2 = jnp.arange(128)[None, :] < _lenS2[:, None]
        _causal = jnp.tril(jnp.ones((128, 128), dtype=bool))
        mask_Bx4096x4096_ik1 = jnp.where(jnp.ones((8, 512, 512), dtype=bool), 1, 0).astype(jnp.int32)
        return (x, condB_coeff, itok_B_0_2, itok_B_14_62, itok_B_3_7, mask_Bx4096x4096_ik1)
    x, condB_coeff, itok_B_0_2, itok_B_14_62, itok_B_3_7, mask_Bx4096x4096_ik1 = _rec_inputs()

    def _L0_cond_setup():
        import jax, jax.numpy as jnp
        import numpy as np
        B, S, D_IN, D_OUT = (4, 64, 512, 512)
        key = jax.random.key(seed)
        k1, k2, k3, k4, k5 = jax.random.split(key, 5)
        hidden_states = jax.random.normal(k1, (B, S, D_IN), dtype=jnp.float32)
        W = jax.random.normal(k2, (D_OUT, D_IN), dtype=jnp.float32) * 0.02
        b = jax.random.normal(k3, (D_OUT,), dtype=jnp.float32) * 0.02
        coeff = jax.random.normal(k4, (B,), dtype=jnp.float32) * 0.01
        mask = jax.random.randint(k5, (B, D_IN, D_OUT), 0, 2, dtype=jnp.int32)
        return {'hidden_states': hidden_states, 'W': W, 'b': b, 'coeff': coeff, 'mask': mask}
    _L0_cond_all = _L0_cond_setup()
    _L0_cond_in = {k: v for k, v in _L0_cond_all.items() if k in ('W', 'b')}
    del _L0_cond_all

    def _L1_cond_setup():
        import jax, jax.numpy as jnp
        import numpy as np
        B, S, D_IN, D_OUT = (4, 256, 512, 512)
        R, NUM_LABELERS = (32, 5)
        LORA_SCALING = 16 / 32
        key = jax.random.key(seed)
        k1, k2, k3, k4, k5 = jax.random.split(key, 5)
        x = jax.random.normal(k1, (B, S, D_IN), dtype=jnp.float32)
        labeler_index = jax.random.randint(k2, (B,), 0, NUM_LABELERS, dtype=jnp.int64)
        W = jax.random.normal(k3, (D_OUT, D_IN), dtype=jnp.float32) * 0.02
        lora_A = jax.random.normal(k4, (NUM_LABELERS, D_IN, R), dtype=jnp.float32) * 0.02
        lora_B_w = jax.random.normal(k5, (D_OUT, R), dtype=jnp.float32) * 0.02
        return {'x': x, 'labeler_index': labeler_index, 'W': W, 'lora_A': lora_A, 'lora_B_w': lora_B_w}
    _L1_cond_all = _L1_cond_setup()
    _L1_cond_in = {k: v for k, v in _L1_cond_all.items() if k in ('W', 'lora_A', 'lora_B_w')}
    del _L1_cond_all

    def _L2_cond_setup():
        import jax, jax.numpy as jnp
        import numpy as np
        B, S, D_IN, D_OUT = (4, 256, 512, 512)
        L, R = (64, 16)
        LORA_ALPHA = 32
        LORA_SCALING = LORA_ALPHA / R
        key = jax.random.key(seed)
        k = jax.random.split(key, 6)
        return {'X': jax.random.normal(k[0], (B, S, D_IN), dtype=jnp.float32), 'W': jax.random.normal(k[1], (D_OUT, D_IN), dtype=jnp.float32) * (1.0 / np.sqrt(D_IN)), 'b': jax.random.normal(k[2], (D_OUT,), dtype=jnp.float32), 'lora_A': jax.random.normal(k[3], (L, D_IN, R), dtype=jnp.float32) * (1.0 / np.sqrt(D_IN)), 'lora_B': jax.random.normal(k[4], (L, D_OUT, R), dtype=jnp.float32) * (1.0 / np.sqrt(D_OUT)), 'lora_ids': jax.random.randint(k[5], (B,), 0, L, dtype=jnp.int64)}
    _L2_cond_all = _L2_cond_setup()
    _L2_cond_in = {k: v for k, v in _L2_cond_all.items() if k in ('W', 'b', 'lora_A', 'lora_B')}
    del _L2_cond_all

    def _L3_cond_setup():
        import jax, jax.numpy as jnp
        import numpy as np
        RANK = 16
        ALPHA = 16.0
        SCALING = ALPHA / RANK
        N_ADAPTERS = 8
        IN_F = 512
        OUT_F = 512
        BATCH = 4
        SEQ = 256
        key = jax.random.key(seed)
        kx, ka, kb, ki = jax.random.split(key, 4)
        x = jax.random.normal(kx, (BATCH, SEQ, IN_F), dtype=jnp.float32)
        A = jax.random.normal(ka, (N_ADAPTERS, OUT_F, RANK), dtype=jnp.float32) * 0.02
        B = jax.random.normal(kb, (N_ADAPTERS, RANK, IN_F), dtype=jnp.float32) * 0.02
        adapter_ids = jax.random.randint(ki, (BATCH,), 0, N_ADAPTERS, dtype=jnp.int32)
        return {'x': x, 'A': A, 'B': B, 'adapter_ids': adapter_ids}
    _L3_cond_all = _L3_cond_setup()
    _L3_cond_in = {k: v for k, v in _L3_cond_all.items() if k in ('A', 'B')}
    del _L3_cond_all
    return {'x': x, 'condB_coeff': condB_coeff, 'itok_B_0_2': itok_B_0_2, 'itok_B_14_62': itok_B_14_62, 'itok_B_3_7': itok_B_3_7, 'mask_Bx4096x4096_ik1': mask_Bx4096x4096_ik1, 'L0_cond_W': _L0_cond_in['W'], 'L0_cond_b': _L0_cond_in['b'], 'L1_cond_W': _L1_cond_in['W'], 'L1_cond_lora_A': _L1_cond_in['lora_A'], 'L1_cond_lora_B_w': _L1_cond_in['lora_B_w'], 'L2_cond_W': _L2_cond_in['W'], 'L2_cond_b': _L2_cond_in['b'], 'L2_cond_lora_A': _L2_cond_in['lora_A'], 'L2_cond_lora_B': _L2_cond_in['lora_B'], 'L3_cond_A': _L3_cond_in['A'], 'L3_cond_B': _L3_cond_in['B']}

def reference(x, condB_coeff, itok_B_0_2, itok_B_14_62, itok_B_3_7, mask_Bx4096x4096_ik1, L0_cond_W, L0_cond_b, L1_cond_W, L1_cond_lora_A, L1_cond_lora_B_w, L2_cond_W, L2_cond_b, L2_cond_lora_A, L2_cond_lora_B, L3_cond_A, L3_cond_B):
    import jax
    import jax.numpy as jnp

    def _L0_cond_ref(hidden_states, W, b, coeff, mask):
        import jax, jax.numpy as jnp
        import numpy as np
        B, S, D_IN, D_OUT = (4, 64, 512, 512)
        output = jnp.einsum('bsi,oi->bso', hidden_states, W) + b
        sign = (2 * mask - 1).astype(hidden_states.dtype)
        diff = jnp.einsum('bsi,bio->bso', hidden_states, sign)
        return output + diff * coeff[:, None, None]

    def _L1_cond_ref(x, labeler_index, W, lora_A, lora_B_w):
        import jax, jax.numpy as jnp
        import numpy as np
        B, S, D_IN, D_OUT = (4, 256, 512, 512)
        R, NUM_LABELERS = (32, 5)
        LORA_SCALING = 16 / 32
        base = jnp.einsum('bsi,oi->bso', x, W)
        labelers_A = lora_A[labeler_index]
        low = jnp.einsum('bsi,bir->bsr', x, labelers_A)
        delta = jnp.einsum('bsr,or->bso', low, lora_B_w) * LORA_SCALING
        return base + delta

    def _L2_cond_ref(X, W, b, lora_A, lora_B, lora_ids):
        import jax, jax.numpy as jnp
        import numpy as np
        B, S, D_IN, D_OUT = (4, 256, 512, 512)
        L, R = (64, 16)
        LORA_ALPHA = 32
        LORA_SCALING = LORA_ALPHA / R
        output = jnp.einsum('bsd,od->bso', X, W) + b
        A = lora_A[lora_ids]
        Bm = lora_B[lora_ids]
        inter = jnp.einsum('bwr,bsw->bsr', A, X)
        lora_out = output + jnp.einsum('bsr,bwr->bsw', inter, Bm) * LORA_SCALING
        return lora_out

    def _L3_cond_ref(x, A, B, adapter_ids):
        import jax, jax.numpy as jnp
        import numpy as np
        RANK = 16
        ALPHA = 16.0
        SCALING = ALPHA / RANK
        N_ADAPTERS = 8
        IN_F = 512
        OUT_F = 512
        BATCH = 4
        SEQ = 256
        B_sel = B[adapter_ids]
        A_sel = A[adapter_ids]
        Bx = jnp.einsum('bni,bri->bnr', x, B_sel)
        out = jnp.einsum('bnr,bor->bno', Bx, A_sel)
        return out * SCALING
    x = x + _L0_cond_ref(x, L0_cond_W, L0_cond_b, condB_coeff, mask_Bx4096x4096_ik1)
    x = x + _L1_cond_ref(x, itok_B_0_2, L1_cond_W, L1_cond_lora_A, L1_cond_lora_B_w)
    x = x + _L2_cond_ref(x, L2_cond_W, L2_cond_b, L2_cond_lora_A, L2_cond_lora_B, itok_B_14_62)
    x = x + _L3_cond_ref(x, L3_cond_A, L3_cond_B, itok_B_3_7)
    return x

_drawn_inputs = setup_inputs


def setup_inputs(seed=0):
    import zlib

    import numpy as np

    out = dict(_drawn_inputs(seed))
    spreads = {}
    factors = {'L0_cond_b': 4.209, 'L1_cond_lora_A': 3.335, 'L1_cond_lora_B_w': 3.306}
    for name, (base, spread) in spreads.items():
        noise = np.random.default_rng([zlib.crc32(name.encode()), seed]).standard_normal(out[name].shape)
        drawn = base * np.exp(spread * noise) if base else spread * noise
        out[name] = jnp.asarray(drawn.astype(out[name].dtype))
    for name, factor in factors.items():
        out[name] = (out[name] * factor).astype(out[name].dtype)
    return out
```

```python
from contextlib import ExitStack

import concourse.bass as bass
from concourse import mybir

P = 128
F32 = mybir.dt.float32
F32R = mybir.dt.float32r
I32 = mybir.dt.int32
ALU = mybir.AluOpType
ACT = mybir.ActivationFunctionType


def lora_stack_kernel(nc, x, coeff, idx1, idx2, idx3, mask, w0, b0, w1, a1, b1, w2, b2, a2, bm2, a3, bm3, consts, out):
    B, S, D = x.shape
    C = D // P
    NPAIR = B // 2
    R1 = a1.shape[2]
    R2 = a2.shape[2]
    R3 = bm3.shape[1]
    Q = 4
    SCALE1, SCALE2 = 0.5, 2.0
    W2B = 2 * S
    assert S == P and R1 * Q == P and 2 * R2 * Q == P and 2 * R3 * Q == P

    groups = [("x", 0), ("x", 1)] + [("w0", c) for c in range(C)] + [("w1", c) for c in range(C)]
    groups += [("x1", 0), ("x1", 1)] + [("w2", c) for c in range(C)] + [("b1", 0)]
    groups += [(n, 0) for n in ("b2", "a3", "b3")] + [("x", 2), ("x", 3)]
    for p in range(1, NPAIR):
        groups += [("x1", 2 * p), ("x1", 2 * p + 1)] + [(n, p) for n in ("b2", "a3", "b3")]
        if p + 1 < NPAIR:
            groups += [("x", 2 * p + 2), ("x", 2 * p + 3)]
    number = {g: n for n, g in enumerate(groups)}
    rounded = {g: n for n, g in enumerate([g for g in groups if g[0] != "w0"])}
    lows = [(1, 0), (2, 0)]
    for p in range(2, NPAIR):
        lows += [(3, p - 2), (1, p - 1), (2, p - 1)]
    lows += [(3, NPAIR - 2), (1, NPAIR - 1), (2, NPAIR - 1), (3, NPAIR - 1)]
    low_number = {g: n for n, g in enumerate(lows)}

    raws = [("w", 0), ("m", 0), ("w", 1), ("m", 1), ("w", 2)] + [("m", b) for b in range(2, B)]
    RAW = 4
    raw_number = {g: n for n, g in enumerate(raws)}

    with ExitStack() as ctx:
        def sb(name, shape, dt=F32):
            return ctx.enter_context(nc.sbuf_tensor(name, shape, dt))

        def ps(name, shape):
            return ctx.enter_context(nc.psum_tensor(name, shape, F32))

        def sem(name):
            return ctx.enter_context(nc.semaphore(name))

        const_sb = sb("const_sb", [P, P + W2B])
        ident = const_sb[:, 0:P]
        pairmask = const_sb[:, P:P + W2B]
        ident_r = sb("ident_r", [P, P], F32R)
        idx_sb = sb("idx_sb", [1, 3 * B], I32)
        coeff_sb = sb("coeff_sb", [P, B])
        coeff2 = sb("coeff2", [P, B])
        ncoeff = sb("ncoeff", [P, B])
        xsum = sb("xsum", [P, B])
        b0_sb = sb("b0_sb", [P, D])
        b2_sb = sb("b2_sb", [P, C])
        junk = sb("junk", [P, D], mybir.dt.bfloat16)
        raw = [sb(f"raw{i}", [P, C, D]) for i in range(RAW)]
        x_in = [sb(f"x_in{i}", [P, 2, D]) for i in range(2)]
        a1_in = sb("a1_in", [P, C, 4, R1])
        a2_in = sb("a2_in", [P, C, 4, R2])
        bm2_in = sb("bm2_in", [P, 4, C, R2])
        a3_in = sb("a3_in", [P, 4, C, R3])
        bm3_in = sb("bm3_in", [2 * R3, 2, D])
        b1_in = sb("b1_in", [P, C, R1])
        turn_b = sb("turn_b", [P, C, Q, 2, R2])
        turn_a = sb("turn_a", [P, C, Q, 2, R3])
        w0t = sb("w0t", [P, C, D])
        w1t = [sb(f"w1t_{s}", [P, C, D], F32R) for s in ("hi", "lo")]
        w2t = [sb(f"w2t_{s}", [P, C, D], F32R) for s in ("hi", "lo")]
        e_sum_sb = sb("e_sum_sb", [P, C, D])
        e_hi_sb = [sb(f"e_hi{i}", [P, C, D], F32R) for i in range(2)]
        e_lo_sb = [sb(f"e_lo{i}", [P, C, D], F32R) for i in range(2)]
        xt = [[sb(f"xt{i}_{s}", [P, C, S], F32R) for s in ("hi", "lo")] for i in range(2)]
        x1_sb = [sb(f"x1_{i}", [P, D]) for i in range(2)]
        x1t = [sb(f"x1t_{s}", [P, C, W2B], F32R) for s in ("hi", "lo")]
        x2t = [sb(f"x2t_{s}", [P, C, W2B], F32R) for s in ("hi", "lo")]
        x3t = [sb(f"x3t_{s}", [P, C, W2B], F32R) for s in ("hi", "lo")]
        a1_st = [sb(f"a1_st{i}", [P, C, 2, Q, R1], F32R) for i in range(2)]
        a2_st = [sb(f"a2_st{i}", [P, C, Q, 2 * R2], F32R) for i in range(2)]
        b3_st = [sb(f"b3_st{i}", [P, C, Q, 2 * R3], F32R) for i in range(2)]
        b1_st = sb("b1_st", [P, D], F32R)
        b2_st = [sb(f"b2_st{i}", [P, D], F32R) for i in range(2)]
        a3_st = [sb(f"a3_st{i}", [P, D], F32R) for i in range(2)]
        low_sb = sb("low_sb", [P, W2B], F32R)
        out_sb = [sb(f"out_sb{i}", [P, D]) for i in range(2)]

        ps_a = [ps(f"ps_a{i}", [P, D]) for i in range(2)]
        ps_t = [ps(f"ps_t{i}", [P, C, P]) for i in range(2)]
        ps_l = ps("ps_l", [P, C, W2B])
        ps_low = ps("ps_low", [P, D])
        ps_o = ps("ps_o", [P, D])

        const_in = sem("const_in")
        small_in = sem("small_in")
        idx_in = sem("idx_in")
        raw_in = [sem(f"raw_in{i}") for i in range(RAW)]
        x_arrived = [sem(f"x_arrived{i}") for i in range(2)]
        b1_arrived = sem("b1_arrived")
        picked = [sem(f"picked{p}") for p in range(NPAIR)]
        staged = sem("staged")
        diag_added = sem("diag_added")
        ident_ready = sem("ident_ready")
        coeff_ready = sem("coeff_ready")
        stack_hi = sem("stack_hi")
        stack_done = sem("stack_done")
        xsum_done = sem("xsum_done")
        tr_ready = sem("tr_ready")
        tr_hi = sem("tr_hi")
        tr_done = sem("tr_done")
        e_sum = sem("e_sum")
        e_hi = sem("e_hi")
        e_split = sem("e_split")
        a_ready = sem("a_ready")
        x1_done = sem("x1_done")
        low_ready = sem("low_ready")
        low_hi = sem("low_hi")
        low_done = sem("low_done")
        l_ready = sem("l_ready")
        l_hi = sem("l_hi")
        l_done = sem("l_done")
        o_ready = sem("o_ready")
        o_even = sem("o_even")
        o_odd = sem("o_odd")
        out_sent = [sem(f"out_sent{i}") for i in range(2)]

        block = ctx.enter_context(nc.Block())

        @block.sync
        def _(sp):
            def load_raw(kind, n):
                i = raw_number[kind, n]
                if i >= RAW:
                    was, m = raws[i - RAW]
                    if was == "m":
                        sp.wait_ge(e_sum, 2 * m + 2)
                    else:
                        sp.wait_ge(tr_ready, number[f"w{m}", C - 1] + 1)
                if kind == "w":
                    src, dst = (w0, w1, w2)[n], raw[i % RAW][:, :, :]
                else:
                    src, dst = mask[n], raw[i % RAW][:, :, :].bitcast(I32)
                sp.dma_start(dst, src.rearrange("(c p) n -> p c n", p=P)).then_inc(raw_in[i % RAW], 16)

            def load_x(p):
                if p >= 2:
                    sp.wait_ge(tr_ready, number["x", 2 * p - 3] + 1)
                    sp.wait_ge(xsum_done, 2 * p - 2)
                sp.dma_start(x_in[p % 2][:, :, :],
                             x[2 * p:2 * p + 2].rearrange("b s d -> s b d")).then_inc(x_arrived[p % 2], 16)

            def pick(p):
                if p >= 2:
                    sp.wait_ge(tr_ready, number["b3", p - 2] + 1)
                    sp.wait_ge(stack_done, 3 * p - 3)
                for b in (2 * p, 2 * p + 1):
                    def index(k, n):
                        return sp.value_load(idx_sb[0:1, k * B + b:k * B + b + 1], min_val=0, max_val=n - 1)

                    i1 = index(0, a1.shape[0])
                    sp.dma_start(a1_in[:, :, b % 4, :],
                                 a1[bass.ds(i1, 1)].rearrange("l (c p) r -> p (l c) r", p=P)).then_inc(picked[p], 16)
                    i2 = index(1, a2.shape[0])
                    sp.dma_start(a2_in[:, :, b % 4, :],
                                 a2[bass.ds(i2, 1)].rearrange("l (c p) r -> p (l c) r", p=P)).then_inc(picked[p], 16)
                    sp.dma_start(bm2_in[:, b % 4, :, :],
                                 bm2[bass.ds(i2, 1)].rearrange("l (p c) r -> p (l c) r", p=P)).then_inc(picked[p], 16)
                    i3 = index(2, a3.shape[0])
                    sp.dma_start(a3_in[:, b % 4, :, :],
                                 a3[bass.ds(i3, 1)].rearrange("l (p c) r -> p (l c) r", p=P)).then_inc(picked[p], 16)
                    sp.dma_start(bm3_in[R3 * (b % 2):R3 * (b % 2) + R3, p % 2, :],
                                 bm3[bass.ds(i3, 1)].rearrange("l r i -> (l r) i")).then_inc(picked[p], 16)

            sp.dma_start(const_sb[:, :], consts).then_inc(const_in, 16)
            load_x(0)
            load_raw("w", 0)
            load_raw("m", 0)
            for k, src in enumerate((idx1, idx2, idx3)):
                sp.dma_start(idx_sb[0:1, k * B:(k + 1) * B], src.rearrange("(a n) -> a n", a=1)).then_inc(idx_in, 16)
            load_raw("w", 1)
            sp.dma_start(b1_in[:, :, :], b1.rearrange("(p c) r -> p c r", p=P)).then_inc(b1_arrived, 16)
            load_raw("m", 1)
            sp.wait_ge(idx_in, 48)
            pick(0)
            load_raw("w", 2)
            load_x(1)
            load_raw("m", 2)
            pick(1)
            load_raw("m", 3)
            for p in range(2, NPAIR):
                load_x(p)
                pick(p)
                load_raw("m", 2 * p)
                load_raw("m", 2 * p + 1)
            for b in range(B):
                sp.wait_ge((o_even, o_odd)[b % 2], b // 2 + 1)
                sp.dma_start(out[b], out_sb[b % 2][:, :]).then_inc(out_sent[b % 2], 16)
            for i in range(2):
                sp.wait_ge(out_sent[i], 16 * NPAIR)

        @block.gpsimd
        def _(pool):
            pool.dma_start(coeff_sb[:, :], coeff.partition_broadcast(P)).then_inc(small_in, 16)
            pool.dma_start(b0_sb[:, :], b0.partition_broadcast(P)).then_inc(small_in, 16)
            pool.dma_start(b2_sb[:, :], b2.rearrange("(c p) -> p c", p=P),
                           allow_slow_non_contiguous=True).then_inc(small_in, 16)
            pool.wait_ge(const_in, 16)
            for n in range(3):
                i = raw_number["w", n]
                pool.wait_ge(raw_in[i % RAW], 16 * (i // RAW + 1))
                for c in range(C):
                    d = raw[i % RAW][:, c, c * P:(c + 1) * P]
                    last = nc.gpsimd.tensor_tensor(d, d, ident, ALU.add)
                last.then_inc(diag_added, 1)
            pool.wait_ge(b1_arrived, 16)
            nc.gpsimd.tensor_copy(turn_b[:, :, :, :, :].rearrange("p c q b r -> p c q (b r)"),
                                  b1_in[:, :, :].unsqueeze(2).broadcast_to([P, C, Q, R1])).then_inc(staged, 1)
            for p in range(NPAIR):
                pool.wait_ge(picked[p], 16 * 10)
                pair = slice(p % 2 * 2, p % 2 * 2 + 2)
                for dst, src, last_group in ((turn_b, bm2_in, ("b2", p - 1) if p else ("b1", 0)),
                                             (turn_a, a3_in, ("a3", p - 1) if p else None)):
                    if last_group:
                        pool.wait_ge(tr_ready, number[last_group] + 1)
                    for c in range(C):
                        last = nc.gpsimd.tensor_copy(dst[:, c, :, :, :],
                                                     src[:, pair, c, :].unsqueeze(1).broadcast_to([P, Q, 2, R2]))
                    last.then_inc(staged, 1)
                if p >= 2:
                    pool.wait_ge(l_ready, 4 * (p - 2) + 4)
                a1s, a2s = a1_st[p % 2], a2_st[p % 2]
                for b in range(2):
                    src = a1_in[:, :, p % 2 * 2 + b, :]
                    nc.gpsimd.tensor_copy(a1s[:, :, b, 0:Q - 1, :],
                                          src.unsqueeze(2).broadcast_to([P, C, Q - 1, R1])).then_inc(stack_hi, 1)
                src2 = a2_in[:, :, pair, :].rearrange("p c b r -> p c (b r)")
                nc.gpsimd.tensor_copy(a2s[:, :, 0:Q - 1, :],
                                      src2.unsqueeze(2).broadcast_to([P, C, Q - 1, 2 * R2])).then_inc(stack_hi, 1)
                pool.wait_ge(stack_hi, 3 * p + 3)
                for b in range(2):
                    nc.gpsimd.tensor_tensor(a1s[:, :, b, Q - 1, :], a1_in[:, :, p % 2 * 2 + b, :],
                                            a1s[:, :, b, 0, :].bitcast(F32), ALU.subtract).then_inc(stack_done, 1)
                nc.gpsimd.tensor_tensor(a2s[:, :, Q - 1, :], src2, a2s[:, :, 0, :].bitcast(F32),
                                        ALU.subtract).then_inc(stack_done, 1)

        @block.tensor
        def _(pe):
            def group(g, blocks):
                n = number[g]
                if n >= 2:
                    pe.wait_ge(tr_done, n - 1)
                for m, cols, src in blocks:
                    last = pe.transpose(ps_t[n % 2][0:m, cols[0], 0:cols[1]], src, ident[0:cols[1], 0:cols[1]])
                last.then_inc(tr_ready, 1)

            def x_turn(b):
                pe.wait_ge(x_arrived[b // 2 % 2], 16 * (b // 4 + 1))
                group(("x", b), [(P, (c, P), x_in[b // 2 % 2][:, b % 2, c * P:(c + 1) * P]) for c in range(C)])

            def w_turn(k):
                r = raw[raw_number["w", k] % RAW]
                pe.wait_ge(diag_added, k + 1)
                for c in range(C):
                    group((f"w{k}", c), [(P, (o, P), r[:, o, c * P:(c + 1) * P]) for o in range(C)])

            def x1_turn(b):
                pe.wait_ge(x1_done, b + 1)
                group(("x1", b), [(P, (c, P), x1_sb[b % 2][:, c * P:(c + 1) * P]) for c in range(C)])

            def adapters_turn(p):
                pe.wait_ge(staged, 2 * p + 3)
                group(("b2", p), [(P, (c, P), turn_b[:, c, :, :, :]) for c in range(C)])
                group(("a3", p), [(P, (c, P), turn_a[:, c, :, :, :]) for c in range(C)])
                pe.wait_ge(picked[p], 16 * 10)
                group(("b3", p), [(P, (c, 2 * R3), bm3_in[:, p % 2, c * P:(c + 1) * P]) for c in range(C)])

            def natural(b):
                pe.wait_ge(tr_done, number["x", b] + 1)
                if b >= 2:
                    pe.wait_ge(x1_done, b - 1)
                if b % 2 and b >= 5:
                    pe.wait_ge(o_odd, b // 2 - 1)
                xh, xl = xt[b % 2]
                eh, el = e_hi_sb[b % 2], e_lo_sb[b % 2]
                for c in range(C):
                    if c % 2 == 0:
                        pe.wait_ge(e_split, 2 * b + c // 2 + 1)
                    pe.matmul(ps_a[b % 2][:, :], xh[:, c, :], eh[:, c, :], start=(c == 0), stop=False)
                    pe.matmul(ps_a[b % 2][:, :], xl[:, c, :], eh[:, c, :], start=False, stop=False)
                    last = pe.matmul(ps_a[b % 2][:, :], xh[:, c, :], el[:, c, :], start=False, stop=(c == C - 1))
                last.then_inc(a_ready, 1)

            def low(layer, p, src, stack):
                n = low_number[layer, p]
                if n:
                    pe.wait_ge(low_done, n)
                if layer == 1:
                    for b in range(2):
                        cols = slice(b * S, (b + 1) * S)
                        for c in range(C):
                            for s in range(2):
                                last = pe.matmul(ps_low[:, cols], stack[:, c, b, :, :], src[s][:, c, cols],
                                                 start=(c == 0 and s == 0), stop=(c == C - 1 and s == 1))
                else:
                    for c in range(C):
                        for s in range(2):
                            last = pe.matmul(ps_low[:, 0:W2B], stack[:, c, :, :], src[s][:, c, :],
                                             start=(c == 0 and s == 0), stop=(c == C - 1 and s == 1))
                last.then_inc(low_ready, 1)

            def turned(layer, p, src, w, second):
                f = 2 * p + layer - 1
                for o in range(C):
                    if o % 2 == 0 and f:
                        pe.wait_ge(l_done, 2 * f - 1 + o // 2)
                    cols = slice(o * P, (o + 1) * P)
                    for c in range(C):
                        pe.matmul(ps_l[:, o, :], w[0][:, c, cols], src[0][:, c, :], start=(c == 0), stop=False)
                        pe.matmul(ps_l[:, o, :], w[0][:, c, cols], src[1][:, c, :], start=False, stop=False)
                        pe.matmul(ps_l[:, o, :], w[1][:, c, cols], src[0][:, c, :], start=False, stop=False)
                    if o == 0:
                        pe.wait_ge(low_done, low_number[layer, p] + 1)
                    last = pe.matmul(ps_l[:, o, :], second[:, cols], low_sb[:, :], start=False, stop=True)
                    if o % 2:
                        last.then_inc(l_ready, 1)

            def layer1(p):
                pe.wait_ge(tr_done, number["x1", 2 * p + 1] + 1)
                pe.wait_ge(stack_done, 3 * p + 3)
                pe.wait_ge(tr_done, number["b1", 0] + 1)
                low(1, p, x1t, a1_st[p % 2])
                turned(1, p, x1t, w1t, b1_st)

            def layer2(p):
                pe.wait_ge(l_done, 4 * p + 2)
                pe.wait_ge(tr_done, number["b3", p] + 1)
                low(2, p, x2t, a2_st[p % 2])
                turned(2, p, x2t, w2t, b2_st[p % 2])

            def layer3(p):
                pe.wait_ge(l_done, 4 * p + 4)
                low(3, p, x3t, b3_st[p % 2])
                for b in range(2):
                    if b == 0 and p:
                        pe.wait_ge(o_even, p)
                    if b == 1:
                        pe.wait_ge(x1_done, min(2 * p + 4, B))
                        if p:
                            pe.wait_ge(o_odd, p)
                    bank = (ps_o, ps_a[1])[b]
                    rows = slice(b * S, (b + 1) * S)
                    for c in range(C):
                        for s in range(2):
                            pe.matmul(bank[:, c * P:(c + 1) * P], x3t[s][:, c, rows], ident_r[:, :],
                                      start=(c == 0 and s == 0), stop=False, skip_group_check=True)
                    if b == 0:
                        pe.wait_ge(low_done, low_number[3, p] + 1)
                    pe.matmul(bank[:, :], low_sb[:, rows], a3_st[p % 2][:, :], start=False, stop=True,
                              skip_group_check=True).then_inc(o_ready, 1)

            pe.wait_ge(const_in, 16)
            x_turn(0)
            x_turn(1)
            w_turn(0)
            w_turn(1)
            natural(0)
            x1_turn(0)
            natural(1)
            x1_turn(1)
            w_turn(2)
            pe.wait_ge(staged, 1)
            group(("b1", 0), [(P, (c, P), turn_b[:, c, :, :, :]) for c in range(C)])
            adapters_turn(0)
            x_turn(2)
            x_turn(3)
            pe.wait_ge(ident_ready, 1)
            for p in range(1, NPAIR):
                natural(2 * p)
                if p >= 2:
                    layer3(p - 2)
                layer1(p - 1)
                x1_turn(2 * p)
                natural(2 * p + 1)
                layer2(p - 1)
                x1_turn(2 * p + 1)
                adapters_turn(p)
                if p + 1 < NPAIR:
                    x_turn(2 * p + 2)
                    x_turn(2 * p + 3)
            layer3(NPAIR - 2)
            layer1(NPAIR - 1)
            layer2(NPAIR - 1)
            layer3(NPAIR - 1)

        @block.scalar
        def _(act):
            def round_group(g, dst, view=None, scale=1.0):
                act.wait_ge(tr_ready, number[g] + 1)
                src = ps_t[number[g] % 2][:, :, :] if view is None else view(ps_t[number[g] % 2])
                act.activation(dst, src, ACT.Copy, scale=scale).then_inc(tr_hi, 1)

            def x_round(b):
                act.wait_ge(x_arrived[b // 2 % 2], 16 * (b // 4 + 1))
                act.wait_ge(coeff_ready, 2)
                if b:
                    act.wait_ge(xsum_done, b)
                act.activation(junk[:, :], x_in[b // 2 % 2][:, b % 2, :], ACT.Copy, scale=ncoeff[:, b:b + 1],
                               accum_out=xsum[:, b:b + 1]).then_inc(xsum_done, 1)
                if b >= 2:
                    act.wait_ge(a_ready, b - 1)
                round_group(("x", b), xt[b % 2][0][:, :, :])

            def e_round(b):
                for h in range(2):
                    act.wait_ge(e_sum, 2 * b + h + 1)
                    if b >= 2:
                        act.wait_ge(a_ready, b - 1)
                    part = slice(2 * h, 2 * h + 2)
                    act.activation(e_hi_sb[b % 2][:, part, :], e_sum_sb[:, part, :], ACT.Copy).then_inc(e_hi, 1)

            def x1_round(b):
                round_group(("x1", b), x1t[0][:, :, (b % 2) * S:(b % 2 + 1) * S])

            def natural_order(t):
                return t[:, :, :].rearrange("k c q -> k q c")

            def adapters_round(p):
                for name, dst, scale in (("b2", b2_st, SCALE2), ("a3", a3_st, 1.0)):
                    round_group((name, p), dst[p % 2][:, :].rearrange("k (q c) -> k q c", c=C), natural_order, scale)
                round_group(("b3", p), b3_st[p % 2][:, :, 0:Q - 1, :],
                            lambda t: t[:, :, 0:2 * R3].unsqueeze(2).broadcast_to([P, C, Q - 1, 2 * R3]))

            def layer1_round(p):
                for j in range(2):
                    act.wait_ge(l_ready, 4 * p + j + 1)
                    act.activation(x2t[0][:, 2 * j:2 * j + 2, :], ps_l[:, 2 * j:2 * j + 2, :], ACT.Copy).then_inc(l_hi, 1)

            def layer2_round(p):
                for o in range(C):
                    act.wait_ge(l_ready, 4 * p + 2 + o // 2 + 1)
                    last = act.activation(x3t[0][:, o, :], ps_l[:, o, :], ACT.Identity, bias=b2_sb[:, o:o + 1])
                    if o % 2:
                        last.then_inc(l_hi, 1)

            def even_out(p):
                act.wait_ge(o_ready, 2 * p + 1)
                if p:
                    act.wait_ge(out_sent[0], 16 * p)
                act.activation(out_sb[0][:, :], ps_o[:, :], ACT.Copy).then_inc(o_even, 1)

            act.wait_ge(const_in, 16)
            act.activation(ident_r[:, :], ident, ACT.Copy).then_inc(ident_ready, 1)
            act.wait_ge(small_in, 48)
            x_round(0)
            x_round(1)
            e_round(0)
            for c in range(C):
                round_group(("w1", c), w1t[0][:, c, :].rearrange("p (o q) -> p o q", o=C))
            x1_round(0)
            e_round(1)
            x1_round(1)
            for c in range(C):
                round_group(("w2", c), w2t[0][:, c, :].rearrange("p (o q) -> p o q", o=C))
            round_group(("b1", 0), b1_st[:, :].rearrange("k (q c) -> k q c", c=C), natural_order, SCALE1)
            adapters_round(0)
            x_round(2)
            x_round(3)
            e_round(2)
            for p in range(1, NPAIR):
                e_round(2 * p + 1)
                if p >= 2:
                    even_out(p - 2)
                layer1_round(p - 1)
                x1_round(2 * p)
                if p + 1 < NPAIR:
                    e_round(2 * p + 2)
                layer2_round(p - 1)
                x1_round(2 * p + 1)
                adapters_round(p)
                if p + 1 < NPAIR:
                    x_round(2 * p + 2)
                    x_round(2 * p + 3)
            even_out(NPAIR - 2)
            layer1_round(NPAIR - 1)
            layer2_round(NPAIR - 1)
            even_out(NPAIR - 1)

        @block.vector
        def _(dve):
            def rest_group(g, dst, hi, view=None, scale=1.0):
                dve.wait_ge(tr_hi, rounded[g] + 1)
                src = ps_t[number[g] % 2][:, :, :] if view is None else view(ps_t[number[g] % 2])
                if scale == 1.0:
                    op = dve.tensor_tensor(dst, src, hi.bitcast(F32), ALU.subtract)
                else:
                    op = dve.scalar_tensor_tensor(dst, src, scale, hi.bitcast(F32), ALU.mult, ALU.subtract)
                op.then_inc(tr_done, 1)

            def x_rest(b):
                rest_group(("x", b), xt[b % 2][1][:, :, :], xt[b % 2][0][:, :, :])

            def e_build(b):
                i = raw_number["m", b]
                dve.wait_ge(raw_in[i % RAW], 16 * (i // RAW + 1))
                for h in range(2):
                    part = slice(2 * h, 2 * h + 2)
                    if b:
                        dve.wait_ge(e_hi, 2 * b - 1 + h)
                        dve.wait_ge(e_split, 2 * b - 1 + h)
                    dve.scalar_tensor_tensor(e_sum_sb[:, part, :], raw[i % RAW][:, part, :].bitcast(I32),
                                             coeff2[:, b:b + 1], w0t[:, part, :], ALU.mult, ALU.add)\
                        .then_inc(e_sum, 1)
                for h in range(2):
                    part = slice(2 * h, 2 * h + 2)
                    dve.wait_ge(e_hi, 2 * b + h + 1)
                    dve.tensor_tensor(e_lo_sb[b % 2][:, part, :], e_sum_sb[:, part, :],
                                      e_hi_sb[b % 2][:, part, :].bitcast(F32), ALU.subtract).then_inc(e_split, 1)

            def x1_take(b):
                dve.wait_ge(a_ready, b + 1)
                dve.wait_ge(xsum_done, b + 1)
                if b >= 2:
                    dve.wait_ge(tr_ready, number["x1", b - 2] + 1)
                dve.scalar_tensor_tensor(x1_sb[b % 2][:, :], ps_a[b % 2][:, :], xsum[:, b:b + 1], b0_sb[:, :],
                                         ALU.add, ALU.add).then_inc(x1_done, 1)

            def x1_rest(b):
                cols = slice((b % 2) * S, (b % 2 + 1) * S)
                rest_group(("x1", b), x1t[1][:, :, cols], x1t[0][:, :, cols])

            def natural_order(rows):
                return lambda t: t[rows, :, :].rearrange("k c q -> k q c")

            def third_rows(t, g, scale):
                rows = slice(2 * R1, 3 * R1)
                part = t[rows, :].rearrange("k (q c) -> k q c", c=C)
                rest_group(g, part, part, natural_order(rows), scale)

            def adapters_rest(p):
                third_rows(b2_st[p % 2], ("b2", p), SCALE2)
                third_rows(a3_st[p % 2], ("a3", p), 1.0)
                rest_group(("b3", p), b3_st[p % 2][:, :, Q - 1, :], b3_st[p % 2][:, :, 0, :],
                           lambda t: t[:, :, 0:2 * R3])

            def low_take(layer, p):
                n = low_number[layer, p]
                dve.wait_ge(low_ready, n + 1)
                rows = slice(R1, 2 * R1)
                if layer == 1:
                    dve.tensor_copy(low_sb[:, :], ps_low[:, 0:W2B]).then_inc(low_hi, 1)
                    dve.wait_ge(low_hi, n + 1)
                    dve.tensor_tensor(low_sb[rows, :], ps_low[rows, 0:W2B], low_sb[rows, :].bitcast(F32),
                                      ALU.subtract).then_inc(low_done, 1)
                    return
                dve.tensor_tensor(low_sb[:, :], ps_low[:, 0:W2B], pairmask, ALU.mult).then_inc(low_hi, 1)
                dve.wait_ge(low_hi, n + 1)
                for b in range(2):
                    cols = slice(b * S, (b + 1) * S)
                    last = dve.scalar_tensor_tensor(low_sb[rows, cols], ps_low[rows, cols],
                                                    pairmask[rows, b * S:b * S + 1], low_sb[rows, cols].bitcast(F32),
                                                    ALU.mult, ALU.subtract)
                last.then_inc(low_done, 1)

            def layer1_rest(p):
                for j in range(2):
                    dve.wait_ge(l_hi, 4 * p + j + 1)
                    half = slice(2 * j, 2 * j + 2)
                    dve.tensor_tensor(x2t[1][:, half, :], ps_l[:, half, :], x2t[0][:, half, :].bitcast(F32),
                                      ALU.subtract).then_inc(l_done, 1)

            def layer2_rest(p):
                for o in range(C):
                    dve.wait_ge(l_hi, 4 * p + 2 + o // 2 + 1)
                    last = dve.scalar_tensor_tensor(x3t[1][:, o, :], ps_l[:, o, :], b2_sb[:, o:o + 1],
                                                    x3t[0][:, o, :].bitcast(F32), ALU.add, ALU.subtract)
                    if o % 2:
                        last.then_inc(l_done, 1)

            def odd_out(p):
                dve.wait_ge(o_ready, 2 * p + 2)
                if p:
                    dve.wait_ge(out_sent[1], 16 * p)
                dve.tensor_copy(out_sb[1][:, :], ps_a[1][:, :]).then_inc(o_odd, 1)

            dve.wait_ge(small_in, 48)
            dve.tensor_scalar(ncoeff[:, :], coeff_sb[:, :], -1.0, None, ALU.mult).then_inc(coeff_ready, 1)
            dve.tensor_scalar(coeff2[:, :], coeff_sb[:, :], 2.0, None, ALU.mult).then_inc(coeff_ready, 1)
            dve.wait_ge(coeff_ready, 2)
            x_rest(0)
            x_rest(1)
            for c in range(C):
                dve.wait_ge(tr_ready, number["w0", c] + 1)
                dve.tensor_copy(w0t[:, c, :].rearrange("p (o q) -> p o q", o=C),
                                ps_t[number["w0", c] % 2][:, :, :]).then_inc(tr_done, 1)
            dve.wait_ge(tr_done, number["w0", C - 1] + 1)
            e_build(0)
            for c in range(C):
                rest_group(("w1", c), w1t[1][:, c, :].rearrange("p (o q) -> p o q", o=C),
                           w1t[0][:, c, :].rearrange("p (o q) -> p o q", o=C))
            x1_take(0)
            x1_rest(0)
            e_build(1)
            x1_take(1)
            x1_rest(1)
            for c in range(C):
                rest_group(("w2", c), w2t[1][:, c, :].rearrange("p (o q) -> p o q", o=C),
                           w2t[0][:, c, :].rearrange("p (o q) -> p o q", o=C))
            third_rows(b1_st, ("b1", 0), SCALE1)
            adapters_rest(0)
            x_rest(2)
            x_rest(3)
            e_build(2)
            for p in range(1, NPAIR):
                e_build(2 * p + 1)
                x1_take(2 * p)
                if p >= 2:
                    low_take(3, p - 2)
                    odd_out(p - 2)
                low_take(1, p - 1)
                layer1_rest(p - 1)
                x1_rest(2 * p)
                if p + 1 < NPAIR:
                    e_build(2 * p + 2)
                x1_take(2 * p + 1)
                low_take(2, p - 1)
                layer2_rest(p - 1)
                x1_rest(2 * p + 1)
                adapters_rest(p)
                if p + 1 < NPAIR:
                    x_rest(2 * p + 2)
                    x_rest(2 * p + 3)
            low_take(3, NPAIR - 2)
            odd_out(NPAIR - 2)
            low_take(1, NPAIR - 1)
            layer1_rest(NPAIR - 1)
            low_take(2, NPAIR - 1)
            layer2_rest(NPAIR - 1)
            low_take(3, NPAIR - 1)
            odd_out(NPAIR - 1)


_INS = ["x", "condB_coeff", "itok_B_0_2", "itok_B_14_62", "itok_B_3_7", "mask_Bx4096x4096_ik1",
        "L0_cond_W", "L0_cond_b", "L1_cond_W", "L1_cond_lora_A", "L1_cond_lora_B_w",
        "L2_cond_W", "L2_cond_b", "L2_cond_lora_A", "L2_cond_lora_B", "L3_cond_A", "L3_cond_B"]


def kernel(**inputs):
    import numpy as _np
    import concourse.bacc as _bacc
    from concourse import mybir as _mybir
    from concourse.bass_utils import run_bass_kernel_spmd as _run

    nc = _bacc.Bacc("TRN2", target_bir_lowering=False, num_devices=1)
    arrays, args = {}, []
    for name in _INS:
        a = _np.ascontiguousarray(inputs[name])
        arrays[f"in_{name}_dram"] = a
        args.append(nc.dram_tensor(f"in_{name}_dram", a.shape, _mybir.dt.from_np(a.dtype), kind="ExternalInput").ap())
    rows, half = _np.arange(128) // 16 % 2, _np.arange(256) // 128
    consts = _np.concatenate([_np.eye(128, dtype=_np.float32),
                              (rows[:, None] == half[None, :]).astype(_np.float32)], axis=1)
    arrays["consts_dram"] = _np.ascontiguousarray(consts)
    args.append(nc.dram_tensor("consts_dram", consts.shape, _mybir.dt.float32, kind="ExternalInput").ap())
    args.append(nc.dram_tensor("out_dram", (8, 128, 512), _mybir.dt.float32, kind="ExternalOutput").ap())
    lora_stack_kernel(nc, *args)
    r = _run(nc, [arrays], core_ids=[0])
    return r.results[0]["out_dram"]
```

```python
from contextlib import ExitStack

import concourse.bass as bass
from concourse import mybir

P = 128
F32 = mybir.dt.float32
F32R = mybir.dt.float32r
I32 = mybir.dt.int32
ALU = mybir.AluOpType
ACT = mybir.ActivationFunctionType


def lora_stack_kernel(nc, x, coeff, idx1, idx2, idx3, mask, w0, b0, w1, a1, b1, w2, b2, a2, bm2, a3, bm3, consts, out):
    B, S, D = x.shape
    C = D // P
    NPAIR = B // 2
    R1 = a1.shape[2]
    R2 = a2.shape[2]
    R3 = bm3.shape[1]
    Q = 4
    SCALE1, SCALE2 = 0.5, 2.0
    W2B = 2 * S
    assert S == P and R1 * Q == P and 2 * R2 * Q == P and 2 * R3 * Q == P

    groups = [("x", 0), ("x", 1)] + [("w0", c) for c in range(C)]
    groups += [("w1", 0), ("w1", 1), ("x1", 0), ("w1", 2), ("w1", 3), ("x1", 1), ("b1", 0)]
    for p in range(NPAIR):
        more = p + 1 < NPAIR
        fill1 = [[("x", 2 * p + 2)] * more, [("b2", p)], [("a3", p)], [("b3", p)]]
        fill2 = [[("x1", 2 * p + 2)] * more, [("x", 2 * p + 3)] * more, [], []]
        for o in range(C):
            groups += fill1[o] + [("w2", o)] * (p == 0)
        for o in range(C):
            groups += fill2[o]
        groups += [("x1", 2 * p + 3)] * more
    number = {g: n for n, g in enumerate(groups)}
    split_number = {g: n for n, g in enumerate([g for g in groups if g[0] != "w0"])}
    low_number = {(layer, p): 3 * p + layer - 1 for p in range(NPAIR) for layer in (1, 2, 3)}

    raws = [("w", 0), ("m", 0), ("m", 1), ("w", 1), ("w", 2)] + [("m", b) for b in range(2, B)]
    RAW = 4
    raw_number = {g: n for n, g in enumerate(raws)}

    with ExitStack() as ctx:
        def sb(name, shape, dt=F32):
            return ctx.enter_context(nc.sbuf_tensor(name, shape, dt))

        def ps(name, shape):
            return ctx.enter_context(nc.psum_tensor(name, shape, F32))

        def sem(name):
            return ctx.enter_context(nc.semaphore(name))

        const_sb = sb("const_sb", [P, P + W2B])
        ident = const_sb[:, 0:P]
        pairmask = const_sb[:, P:P + W2B]
        ident_r = sb("ident_r", [P, P], F32R)
        idx_sb = sb("idx_sb", [1, 3 * B], I32)
        coeff_sb = sb("coeff_sb", [P, B])
        coeff2 = sb("coeff2", [P, B])
        ncoeff = sb("ncoeff", [P, B])
        xsum = sb("xsum", [P, B])
        b0_sb = sb("b0_sb", [P, D])
        b2_sb = sb("b2_sb", [P, C])
        junk = sb("junk", [P, D], mybir.dt.bfloat16)
        raw = [sb(f"raw{i}", [P, C, D]) for i in range(RAW)]
        x_in = [sb(f"x_in{i}", [P, 2, D]) for i in range(2)]
        a1_in = sb("a1_in", [P, C, 4, R1])
        a2_in = sb("a2_in", [P, C, 4, R2])
        bm2_in = sb("bm2_in", [P, C, 4, R2])
        a3_in = sb("a3_in", [P, C, 4, R3])
        bm3_in = sb("bm3_in", [2 * R3, 2, D])
        b1_in = sb("b1_in", [P, C, R1])
        turn_b = sb("turn_b", [P, C, Q, 2 * R2])
        turn_a = sb("turn_a", [P, C, Q, 2 * R3])
        w0t = sb("w0t", [P, C, D])
        w1t = [sb(f"w1t_{s}", [P, C, D], F32R) for s in ("hi", "lo")]
        w2t = [sb(f"w2t_{s}", [P, C, D], F32R) for s in ("hi", "lo")]
        e_sum_sb = sb("e_sum_sb", [P, C, D])
        e_hi_sb = [sb(f"e_hi{i}", [P, C, D], F32R) for i in range(2)]
        e_lo_sb = [sb(f"e_lo{i}", [P, C, D], F32R) for i in range(2)]
        xt = [[sb(f"xt{i}_{s}", [P, C, S], F32R) for s in ("hi", "lo")] for i in range(2)]
        x1_sb = [sb(f"x1_{i}", [P, D]) for i in range(2)]
        x1t = [sb(f"x1t_{s}", [P, C, W2B], F32R) for s in ("hi", "lo")]
        x2t = [sb(f"x2t_{s}", [P, C, W2B], F32R) for s in ("hi", "lo")]
        x3t = [sb(f"x3t_{s}", [P, C, W2B], F32R) for s in ("hi", "lo")]
        a1_st = sb("a1_st", [P, C, 2, Q, R1], F32R)
        a2_st = sb("a2_st", [P, C, Q, 2 * R2], F32R)
        b3_st = sb("b3_st", [P, C, Q, 2 * R3], F32R)
        b1_st = sb("b1_st", [P, D], F32R)
        b2_st = sb("b2_st", [P, D], F32R)
        a3_st = sb("a3_st", [P, D], F32R)
        low_sb = sb("low_sb", [P, W2B], F32R)
        out_sb = [sb(f"out_sb{i}", [P, D]) for i in range(2)]

        ps_a = [ps(f"ps_a{i}", [P, D]) for i in range(2)]
        ps_t = [ps(f"ps_t{i}", [P, C, P]) for i in range(2)]
        ps_l = [ps(f"ps_l{i}", [P, D])[:, 0:W2B] for i in range(2)]
        ps_low = ps("ps_low", [P, D])
        ps_o = ps("ps_o", [P, D])

        const_in = sem("const_in")
        coeff_in = sem("coeff_in")
        bias_in = sem("bias_in")
        idx_in = sem("idx_in")
        raw_in = [sem(f"raw_in{i}") for i in range(RAW)]
        x_arrived = [sem(f"x_arrived{i}") for i in range(2)]
        b1_arrived = sem("b1_arrived")
        picked = [sem(f"picked{p}") for p in range(NPAIR)]
        diag0_added = sem("diag0_added")
        diag_added = sem("diag_added")
        ident_ready = sem("ident_ready")
        coeff_ready = sem("coeff_ready")
        staged = sem("staged")
        a1_hi = sem("a1_hi")
        a2_hi = sem("a2_hi")
        a1_done = sem("a1_done")
        a2_done = sem("a2_done")
        xsum_done = sem("xsum_done")
        tr_ready = sem("tr_ready")
        tr_hi = sem("tr_hi")
        tr_done = sem("tr_done")
        e_sum = sem("e_sum")
        e_hi = sem("e_hi")
        e_lo = [sem("e_lo_dve"), sem("e_lo_pool")]
        a_ready = sem("a_ready")
        x1_done = sem("x1_done")
        low_ready = sem("low_ready")
        low_hi = sem("low_hi")
        low_done = sem("low_done")
        l_ready = sem("l_ready")
        l_hi = sem("l_hi")
        l_done = sem("l_done")
        o_ready = sem("o_ready")
        o_done = sem("o_done")
        out_sent = [sem(f"out_sent{i}") for i in range(2)]

        block = ctx.enter_context(nc.Block())

        @block.sync
        def _(sp):
            def load_raw(kind, n):
                i = raw_number[kind, n]
                if i >= RAW:
                    was, m = raws[i - RAW]
                    if was == "m":
                        sp.wait_ge(e_sum, 2 * m + 2)
                    else:
                        sp.wait_ge(tr_ready, number[f"w{m}", C - 1] + 1)
                if kind == "w":
                    src, dst = (w0, w1, w2)[n], raw[i % RAW][:, :, :]
                else:
                    src, dst = mask[n], raw[i % RAW][:, :, :].bitcast(I32)
                sp.dma_start(dst, src.rearrange("(c p) n -> p c n", p=P)).then_inc(raw_in[i % RAW], 16)

            def load_x(p):
                if p >= 2:
                    sp.wait_ge(tr_ready, number["x", 2 * p - 3] + 1)
                    sp.wait_ge(xsum_done, 2 * p - 2)
                sp.dma_start(x_in[p % 2][:, :, :],
                             x[2 * p:2 * p + 2].rearrange("b s d -> s b d")).then_inc(x_arrived[p % 2], 16)

            def pick(p):
                if p >= 2:
                    sp.wait_ge(tr_ready, number["b3", p - 2] + 1)
                    sp.wait_ge(staged, 2 * p - 1)
                    sp.wait_ge(a1_done, 2 * p - 2)
                    sp.wait_ge(a2_done, p - 1)
                for b in (2 * p, 2 * p + 1):
                    def index(k, n):
                        return sp.value_load(idx_sb[0:1, k * B + b:k * B + b + 1], min_val=0, max_val=n - 1)

                    i1 = index(0, a1.shape[0])
                    sp.dma_start(a1_in[:, :, b % 4, :],
                                 a1[bass.ds(i1, 1)].rearrange("l (c p) r -> p (l c) r", p=P)).then_inc(picked[p], 16)
                    i2 = index(1, a2.shape[0])
                    sp.dma_start(a2_in[:, :, b % 4, :],
                                 a2[bass.ds(i2, 1)].rearrange("l (c p) r -> p (l c) r", p=P)).then_inc(picked[p], 16)
                    sp.dma_start(bm2_in[:, :, b % 4, :],
                                 bm2[bass.ds(i2, 1)].rearrange("l (p c) r -> p (l c) r", p=P)).then_inc(picked[p], 16)
                    i3 = index(2, a3.shape[0])
                    sp.dma_start(a3_in[:, :, b % 4, :],
                                 a3[bass.ds(i3, 1)].rearrange("l (p c) r -> p (l c) r", p=P)).then_inc(picked[p], 16)
                    sp.dma_start(bm3_in[R3 * (b % 2):R3 * (b % 2) + R3, p % 2, :],
                                 bm3[bass.ds(i3, 1)].rearrange("l r i -> (l r) i")).then_inc(picked[p], 16)

            sp.dma_start(const_sb[:, :], consts).then_inc(const_in, 16)
            load_x(0)
            load_raw("w", 0)
            load_raw("m", 0)
            for k, src in enumerate((idx1, idx2, idx3)):
                sp.dma_start(idx_sb[0:1, k * B:(k + 1) * B], src.rearrange("(a n) -> a n", a=1)).then_inc(idx_in, 16)
            load_raw("m", 1)
            load_raw("w", 1)
            sp.dma_start(b1_in[:, :, :], b1.rearrange("(p c) r -> p c r", p=P)).then_inc(b1_arrived, 16)
            sp.wait_ge(idx_in, 48)
            pick(0)
            load_raw("w", 2)
            load_x(1)
            load_raw("m", 2)
            pick(1)
            load_raw("m", 3)
            for p in range(NPAIR):
                if p + 2 < NPAIR:
                    load_x(p + 2)
                    load_raw("m", 2 * p + 4)
                    pick(p + 2)
                    load_raw("m", 2 * p + 5)
                for b in (2 * p, 2 * p + 1):
                    sp.wait_ge(o_done, b + 1)
                    sp.dma_start(out[b], out_sb[b % 2][:, :]).then_inc(out_sent[b % 2], 16)
            for i in range(2):
                sp.wait_ge(out_sent[i], 16 * NPAIR)

        @block.gpsimd
        def _(pool):
            def diagonal(k):
                i = raw_number["w", k]
                pool.wait_ge(raw_in[i % RAW], 16 * (i // RAW + 1))
                for c in range(C):
                    d = raw[i % RAW][:, c, c * P:(c + 1) * P]
                    last = nc.gpsimd.tensor_tensor(d, d, ident, ALU.add)
                last.then_inc(diag_added, 1)

            def e_rest(b):
                pool.wait_ge(e_hi, 2 * b + 2)
                part = slice(C // 2, C)
                nc.gpsimd.tensor_tensor(e_lo_sb[b % 2][:, part, :], e_sum_sb[:, part, :],
                                        e_hi_sb[b % 2][:, part, :].bitcast(F32), ALU.subtract).then_inc(e_lo[1], 1)

            def a1_rest(p):
                for b in range(2):
                    pool.wait_ge(a1_hi, 2 * p + b + 1)
                    nc.gpsimd.tensor_tensor(a1_st[:, :, b, Q - 1, :], a1_in[:, :, p % 2 * 2 + b, :],
                                            a1_st[:, :, b, 0, :].bitcast(F32), ALU.subtract).then_inc(a1_done, 1)

            def a2_rest(p):
                pool.wait_ge(a2_hi, p + 1)
                src = a2_in[:, :, p % 2 * 2:p % 2 * 2 + 2, :].rearrange("p c b r -> p c (b r)")
                nc.gpsimd.tensor_tensor(a2_st[:, :, Q - 1, :], src, a2_st[:, :, 0, :].bitcast(F32),
                                        ALU.subtract).then_inc(a2_done, 1)

            pool.dma_start(coeff_sb[:, :], coeff.partition_broadcast(P)).then_inc(coeff_in, 16)
            pool.dma_start(b0_sb[:, :], b0.partition_broadcast(P)).then_inc(bias_in, 16)
            pool.dma_start(b2_sb[:, :], b2.rearrange("(c p) -> p c", p=P),
                           allow_slow_non_contiguous=True).then_inc(bias_in, 16)
            pool.wait_ge(const_in, 16)
            e_rest(0)
            e_rest(1)
            diagonal(1)
            diagonal(2)
            a1_rest(0)
            a2_rest(0)
            e_rest(2)
            for p in range(NPAIR - 1):
                e_rest(2 * p + 3)
                a1_rest(p + 1)
                if 2 * p + 4 < B:
                    e_rest(2 * p + 4)
                a2_rest(p + 1)

        @block.tensor
        def _(pe):
            def group(g, blocks):
                n = number[g]
                if n >= 2:
                    if groups[n - 2][0] == "w0":
                        pe.wait_ge(tr_hi, n - 1)
                    else:
                        pe.wait_ge(tr_done, split_number[groups[n - 2]] + 1)
                for m, cols, src in blocks:
                    last = pe.transpose(ps_t[n % 2][0:m, cols[0], 0:cols[1]], src, ident[0:cols[1], 0:cols[1]])
                last.then_inc(tr_ready, 1)

            def x_turn(b):
                pe.wait_ge(x_arrived[b // 2 % 2], 16 * (b // 4 + 1))
                group(("x", b), [(P, (c, P), x_in[b // 2 % 2][:, b % 2, c * P:(c + 1) * P]) for c in range(C)])

            def w_turn(k, c):
                r = raw[raw_number["w", k] % RAW]
                if k:
                    pe.wait_ge(diag_added, k)
                else:
                    pe.wait_ge(diag0_added, 1)
                group((f"w{k}", c), [(P, (o, P), r[:, o, c * P:(c + 1) * P]) for o in range(C)])

            def x1_turn(b):
                pe.wait_ge(x1_done, b + 1)
                group(("x1", b), [(P, (c, P), x1_sb[b % 2][:, c * P:(c + 1) * P]) for c in range(C)])

            def columns_turn(name, p, src):
                pe.wait_ge(staged, {"b1": 1, "b2": 2 * p + 2, "a3": 2 * p + 3}[name])
                group((name, p), [(P, (c, P), src[:, c, :, :]) for c in range(C)])

            def b3_turn(p):
                pe.wait_ge(picked[p], 16 * 10)
                group(("b3", p), [(P, (c, 2 * R3), bm3_in[:, p % 2, c * P:(c + 1) * P]) for c in range(C)])

            def natural(b):
                pe.wait_ge(tr_done, split_number["x", b] + 1)
                if b >= 2:
                    pe.wait_ge(x1_done, b - 1)
                if b % 2 == 0 and b >= 4:
                    pe.wait_ge(o_done, b - 2)
                xh, xl = xt[b % 2]
                eh, el = e_hi_sb[b % 2], e_lo_sb[b % 2]
                for c in range(C):
                    if c % 2 == 0:
                        pe.wait_ge(e_lo[c // 2], b + 1)
                    pe.matmul(ps_a[b % 2][:, :], xh[:, c, :], eh[:, c, :], start=(c == 0), stop=False)
                    pe.matmul(ps_a[b % 2][:, :], xl[:, c, :], eh[:, c, :], start=False, stop=False)
                    last = pe.matmul(ps_a[b % 2][:, :], xh[:, c, :], el[:, c, :], start=False, stop=(c == C - 1))
                last.then_inc(a_ready, 1)

            def low(layer, p, src, stack):
                n = low_number[layer, p]
                if n:
                    pe.wait_ge(low_done, n)
                if layer == 1:
                    for b in range(2):
                        if b == 1:
                            pe.wait_ge(tr_done, split_number["x1", 2 * p + 1] + 1)
                        for c in range(C):
                            for s in range(2):
                                last = pe.matmul(ps_low[:, b * S:(b + 1) * S], stack[:, c, b, :, :],
                                                 src[s][:, c, b * S:b * S + S],
                                                 start=(c == 0 and s == 0), stop=(c == C - 1 and s == 1))
                else:
                    for c in range(C):
                        pe.wait_ge(l_done, 8 * p + 4 * (layer - 2) + c + 1)
                        for s in range(2):
                            last = pe.matmul(ps_low[:, 0:W2B], stack[:, c, :, :], src[s][:, c, :],
                                             start=(c == 0 and s == 0), stop=(c == C - 1 and s == 1))
                last.then_inc(low_ready, 1)

            def turned(layer, p, src, w, second, fill):
                f = 2 * p + layer - 1
                for o in range(C):
                    if 4 * f + o >= 2:
                        pe.wait_ge(l_done, 4 * f + o - 1)
                    cols = slice(o * P, (o + 1) * P)
                    for c in range(C):
                        pe.matmul(ps_l[o % 2], w[0][:, c, cols], src[0][:, c, :], start=(c == 0), stop=False)
                        pe.matmul(ps_l[o % 2], w[0][:, c, cols], src[1][:, c, :], start=False, stop=False)
                        pe.matmul(ps_l[o % 2], w[1][:, c, cols], src[0][:, c, :], start=False, stop=False)
                    if o == 0:
                        pe.wait_ge(low_done, low_number[layer, p] + 1)
                    pe.matmul(ps_l[o % 2], second[:, cols], low_sb[:, :], start=False, stop=True)\
                        .then_inc(l_ready, 1)
                    fill(o)

            def layer1(p):
                def fill(o):
                    if o == 0 and p + 1 < NPAIR:
                        x_turn(2 * p + 2)
                    if o == 1:
                        columns_turn("b2", p, turn_b)
                    if o == 2:
                        columns_turn("a3", p, turn_a)
                    if o == 3:
                        b3_turn(p)
                    if p == 0:
                        w_turn(2, o)

                pe.wait_ge(tr_done, split_number["x1", 2 * p] + 1)
                pe.wait_ge(a1_done, 2 * p + 2)
                low(1, p, x1t, a1_st)
                turned(1, p, x1t, w1t, b1_st, fill)

            def layer2(p):
                def fill(o):
                    if o == 0 and p + 1 < NPAIR:
                        x1_turn(2 * p + 2)
                    if o == 1 and p + 1 < NPAIR:
                        x_turn(2 * p + 3)

                pe.wait_ge(tr_done, split_number["b3", p] + 1)
                if p == 0:
                    pe.wait_ge(tr_done, split_number["w2", C - 1] + 1)
                pe.wait_ge(a2_done, p + 1)
                low(2, p, x2t, a2_st)
                turned(2, p, x2t, w2t, b2_st, fill)

            def layer3(p):
                low(3, p, x3t, b3_st)
                banks = (ps_o, ps_a[0])
                if p:
                    pe.wait_ge(o_done, 2 * p)
                pe.wait_ge(x1_done, min(2 * p + 3, B))
                for b in range(2):
                    for c in range(C):
                        for s in range(2):
                            pe.matmul(banks[b][:, c * P:(c + 1) * P], x3t[s][:, c, b * S:(b + 1) * S], ident_r[:, :],
                                      start=(c == 0 and s == 0), stop=False, skip_group_check=True)
                if p + 1 < NPAIR:
                    x1_turn(2 * p + 3)
                pe.wait_ge(low_done, low_number[3, p] + 1)
                for b in range(2):
                    pe.matmul(banks[b][:, :], low_sb[:, b * S:(b + 1) * S], a3_st[:, :], start=False, stop=True,
                              skip_group_check=True).then_inc(o_ready, 1)

            pe.wait_ge(const_in, 16)
            x_turn(0)
            x_turn(1)
            for c in range(C):
                w_turn(0, c)
            natural(0)
            natural(1)
            w_turn(1, 0)
            w_turn(1, 1)
            x1_turn(0)
            w_turn(1, 2)
            w_turn(1, 3)
            x1_turn(1)
            columns_turn("b1", 0, turn_b)
            pe.wait_ge(ident_ready, 1)
            for p in range(NPAIR):
                layer1(p)
                if p + 1 < NPAIR:
                    natural(2 * p + 2)
                layer2(p)
                if p + 1 < NPAIR:
                    natural(2 * p + 3)
                layer3(p)

        @block.scalar
        def _(act):
            def round_group(g, dst, view=None, scale=1.0):
                act.wait_ge(tr_ready, number[g] + 1)
                src = ps_t[number[g] % 2][:, :, :] if view is None else view(ps_t[number[g] % 2])
                act.activation(dst, src, ACT.Copy, scale=scale).then_inc(tr_hi, 1)

            def x_sum(b):
                act.wait_ge(x_arrived[b // 2 % 2], 16 * (b // 4 + 1))
                act.wait_ge(coeff_ready, 2)
                if b:
                    act.wait_ge(xsum_done, b)
                act.activation(junk[:, :], x_in[b // 2 % 2][:, b % 2, :], ACT.Copy, scale=ncoeff[:, b:b + 1],
                               accum_out=xsum[:, b:b + 1]).then_inc(xsum_done, 1)

            def x_round(b):
                if b >= 2:
                    act.wait_ge(a_ready, b - 1)
                round_group(("x", b), xt[b % 2][0][:, :, :])

            def e_round(b, h):
                act.wait_ge(e_sum, 2 * b + h + 1)
                if b >= 2:
                    act.wait_ge(a_ready, b - 1)
                part = slice(2 * h, 2 * h + 2)
                act.activation(e_hi_sb[b % 2][:, part, :], e_sum_sb[:, part, :], ACT.Copy).then_inc(e_hi, 1)

            def x1_round(b):
                round_group(("x1", b), x1t[0][:, :, (b % 2) * S:(b % 2 + 1) * S])

            def natural_order(t):
                return t[:, :, :].rearrange("k c q -> k q c")

            def b2_round(p):
                round_group(("b2", p), b2_st[:, :].rearrange("k (q c) -> k q c", c=C), natural_order, SCALE2)

            def a3_round(p):
                round_group(("a3", p), a3_st[:, :].rearrange("k (q c) -> k q c", c=C), natural_order)

            def b3_round(p):
                round_group(("b3", p), b3_st[:, :, 0:Q - 1, :],
                            lambda t: t[:, :, 0:2 * R3].unsqueeze(2).broadcast_to([P, C, Q - 1, 2 * R3]))

            def block_round(layer, p, o):
                act.wait_ge(l_ready, 8 * p + 4 * (layer - 1) + o + 1)
                if layer == 1:
                    act.activation(x2t[0][:, o, :], ps_l[o % 2], ACT.Copy).then_inc(l_hi, 1)
                else:
                    act.activation(x3t[0][:, o, :], ps_l[o % 2], ACT.Identity, bias=b2_sb[:, o:o + 1])\
                       .then_inc(l_hi, 1)

            def outs(p):
                for b in range(2):
                    act.wait_ge(o_ready, 2 * p + b + 1)
                    if p:
                        act.wait_ge(out_sent[b], 16 * p)
                    act.activation(out_sb[b][:, :], (ps_o, ps_a[0])[b][:, :], ACT.Copy).then_inc(o_done, 1)

            def stage(dst, src, last_group):
                if last_group:
                    act.wait_ge(tr_ready, number[last_group] + 1)
                act.activation(dst[:, :, :, :], src.unsqueeze(2).broadcast_to([P, C, Q, 2 * R2]), ACT.Copy)\
                   .then_inc(staged, 1)

            def pair_of(t, p):
                return t[:, :, p % 2 * 2:p % 2 * 2 + 2, :].rearrange("p c b r -> p c (b r)")

            def adapters_stage(p):
                act.wait_ge(picked[p], 16 * 10)
                stage(turn_b, pair_of(bm2_in, p), ("b2", p - 1) if p else ("b1", 0))
                stage(turn_a, pair_of(a3_in, p), ("a3", p - 1) if p else None)

            def a1_stack(p):
                act.wait_ge(picked[p], 16 * 10)
                if p:
                    act.wait_ge(low_ready, low_number[1, p - 1] + 1)
                for b in range(2):
                    act.activation(a1_st[:, :, b, 0:Q - 1, :],
                                   a1_in[:, :, p % 2 * 2 + b, :].unsqueeze(2).broadcast_to([P, C, Q - 1, R1]),
                                   ACT.Copy).then_inc(a1_hi, 1)

            def a2_stack(p):
                act.wait_ge(picked[p], 16 * 10)
                if p:
                    act.wait_ge(low_ready, low_number[2, p - 1] + 1)
                act.activation(a2_st[:, :, 0:Q - 1, :],
                               pair_of(a2_in, p).unsqueeze(2).broadcast_to([P, C, Q - 1, 2 * R2]),
                               ACT.Copy).then_inc(a2_hi, 1)

            act.wait_ge(const_in, 16)
            act.activation(ident_r[:, :], ident, ACT.Copy).then_inc(ident_ready, 1)
            def w_round(k, w, c):
                round_group((f"w{k}", c), w[:, c, :].rearrange("p (o q) -> p o q", o=C))

            x_round(0)
            x_round(1)
            for c in range(C):
                w_round(0, w0t, c)
            for b in range(2):
                for h in range(2):
                    e_round(b, h)
                x_sum(b)
            act.wait_ge(b1_arrived, 16)
            stage(turn_b, b1_in[:, :, :], None)
            w_round(1, w1t[0], 0)
            w_round(1, w1t[0], 1)
            x1_round(0)
            w_round(1, w1t[0], 2)
            w_round(1, w1t[0], 3)
            x1_round(1)
            round_group(("b1", 0), b1_st[:, :].rearrange("k (q c) -> k q c", c=C), natural_order, SCALE1)
            a1_stack(0)
            adapters_stage(0)
            a2_stack(0)
            act.wait_ge(bias_in, 32)
            for p in range(NPAIR):
                more = p + 1 < NPAIR
                if p == 0:
                    e_round(2, 0)
                    e_round(2, 1)
                if more:
                    x_round(2 * p + 2)
                if p == 0:
                    w_round(2, w2t[0], 0)
                block_round(1, p, 0)
                block_round(1, p, 1)
                b2_round(p)
                if more:
                    e_round(2 * p + 3, 0)
                if p == 0:
                    w_round(2, w2t[0], 1)
                block_round(1, p, 2)
                a3_round(p)
                if p == 0:
                    w_round(2, w2t[0], 2)
                block_round(1, p, 3)
                b3_round(p)
                if more:
                    e_round(2 * p + 3, 1)
                if p == 0:
                    w_round(2, w2t[0], 3)
                if more:
                    x_sum(2 * p + 2)
                    adapters_stage(p + 1)
                    a1_stack(p + 1)
                block_round(2, p, 0)
                if more:
                    x1_round(2 * p + 2)
                block_round(2, p, 1)
                if more:
                    x_round(2 * p + 3)
                if 2 * p + 4 < B:
                    e_round(2 * p + 4, 0)
                block_round(2, p, 2)
                block_round(2, p, 3)
                if 2 * p + 4 < B:
                    e_round(2 * p + 4, 1)
                if more:
                    x_sum(2 * p + 3)
                    a2_stack(p + 1)
                    x1_round(2 * p + 3)
                outs(p)

        @block.vector
        def _(dve):
            def rest_group(g, dst, hi, view=None, scale=1.0):
                dve.wait_ge(tr_hi, number[g] + 1)
                src = ps_t[number[g] % 2][:, :, :] if view is None else view(ps_t[number[g] % 2])
                if scale == 1.0:
                    op = dve.tensor_tensor(dst, src, hi.bitcast(F32), ALU.subtract)
                else:
                    op = dve.scalar_tensor_tensor(dst, src, scale, hi.bitcast(F32), ALU.mult, ALU.subtract)
                op.then_inc(tr_done, 1)

            def x_rest(b):
                rest_group(("x", b), xt[b % 2][1][:, :, :], xt[b % 2][0][:, :, :])

            def e_build(b, h):
                i = raw_number["m", b]
                dve.wait_ge(raw_in[i % RAW], 16 * (i // RAW + 1))
                part = slice(2 * h, 2 * h + 2)
                if b:
                    dve.wait_ge(e_lo[h], b)
                dve.scalar_tensor_tensor(e_sum_sb[:, part, :], raw[i % RAW][:, part, :].bitcast(I32),
                                         coeff2[:, b:b + 1], w0t[:, part, :], ALU.mult, ALU.add).then_inc(e_sum, 1)

            def e_rest(b):
                dve.wait_ge(e_hi, 2 * b + 1)
                part = slice(0, C // 2)
                dve.tensor_tensor(e_lo_sb[b % 2][:, part, :], e_sum_sb[:, part, :],
                                  e_hi_sb[b % 2][:, part, :].bitcast(F32), ALU.subtract).then_inc(e_lo[0], 1)

            def x1_take(b):
                dve.wait_ge(a_ready, b + 1)
                dve.wait_ge(xsum_done, b + 1)
                if b >= 2:
                    dve.wait_ge(tr_ready, number["x1", b - 2] + 1)
                dve.scalar_tensor_tensor(x1_sb[b % 2][:, :], ps_a[b % 2][:, :], xsum[:, b:b + 1], b0_sb[:, :],
                                         ALU.add, ALU.add).then_inc(x1_done, 1)

            def x1_rest(b):
                cols = slice((b % 2) * S, (b % 2 + 1) * S)
                rest_group(("x1", b), x1t[1][:, :, cols], x1t[0][:, :, cols])

            def natural_order(rows):
                return lambda t: t[rows, :, :].rearrange("k c q -> k q c")

            def third_rows(t, g, scale):
                rows = slice(2 * R1, 3 * R1)
                part = t[rows, :].rearrange("k (q c) -> k q c", c=C)
                rest_group(g, part, part, natural_order(rows), scale)

            def b3_rest(p):
                rest_group(("b3", p), b3_st[:, :, Q - 1, :], b3_st[:, :, 0, :], lambda t: t[:, :, 0:2 * R3])

            def low_take(layer, p):
                n = low_number[layer, p]
                dve.wait_ge(low_ready, n + 1)
                rows = slice(R1, 2 * R1)
                if layer == 1:
                    dve.tensor_copy(low_sb[:, :], ps_low[:, 0:W2B]).then_inc(low_hi, 1)
                    dve.wait_ge(low_hi, n + 1)
                    dve.tensor_tensor(low_sb[rows, :], ps_low[rows, 0:W2B], low_sb[rows, :].bitcast(F32),
                                      ALU.subtract).then_inc(low_done, 1)
                    return
                dve.tensor_tensor(low_sb[:, :], ps_low[:, 0:W2B], pairmask, ALU.mult).then_inc(low_hi, 1)
                dve.wait_ge(low_hi, n + 1)
                for b in range(2):
                    cols = slice(b * S, (b + 1) * S)
                    last = dve.scalar_tensor_tensor(low_sb[rows, cols], ps_low[rows, cols],
                                                    pairmask[rows, b * S:b * S + 1], low_sb[rows, cols].bitcast(F32),
                                                    ALU.mult, ALU.subtract)
                last.then_inc(low_done, 1)

            def block_rest(layer, p, o):
                dve.wait_ge(l_hi, 8 * p + 4 * (layer - 1) + o + 1)
                if layer == 1:
                    dve.tensor_tensor(x2t[1][:, o, :], ps_l[o % 2], x2t[0][:, o, :].bitcast(F32),
                                      ALU.subtract).then_inc(l_done, 1)
                else:
                    dve.scalar_tensor_tensor(x3t[1][:, o, :], ps_l[o % 2], b2_sb[:, o:o + 1],
                                             x3t[0][:, o, :].bitcast(F32), ALU.add, ALU.subtract).then_inc(l_done, 1)

            def w_rest(k, w, c):
                rest_group((f"w{k}", c), w[1][:, c, :].rearrange("p (o q) -> p o q", o=C),
                           w[0][:, c, :].rearrange("p (o q) -> p o q", o=C))

            dve.wait_ge(coeff_in, 16)
            dve.tensor_scalar(ncoeff[:, :], coeff_sb[:, :], -1.0, None, ALU.mult).then_inc(coeff_ready, 1)
            dve.tensor_scalar(coeff2[:, :], coeff_sb[:, :], 2.0, None, ALU.mult).then_inc(coeff_ready, 1)
            dve.wait_ge(coeff_ready, 2)
            dve.wait_ge(const_in, 16)
            x_rest(0)
            x_rest(1)
            dve.wait_ge(raw_in[0], 16)
            for c in range(C):
                d = raw[0][:, c, c * P:(c + 1) * P]
                last = dve.tensor_tensor(d, d, ident, ALU.add)
            last.then_inc(diag0_added, 1)
            for b in range(2):
                for h in range(2):
                    if b == 0:
                        dve.wait_ge(tr_hi, number["w0", 2 * h + 1] + 1)
                    e_build(b, h)
                e_rest(b)
            w_rest(1, w1t, 0)
            dve.wait_ge(bias_in, 32)
            x1_take(0)
            w_rest(1, w1t, 1)
            x1_rest(0)
            x1_take(1)
            w_rest(1, w1t, 2)
            w_rest(1, w1t, 3)
            x1_rest(1)
            third_rows(b1_st, ("b1", 0), SCALE1)
            for p in range(NPAIR):
                more = p + 1 < NPAIR
                if p == 0:
                    e_build(2, 0)
                    e_build(2, 1)
                low_take(1, p)
                if p == 0:
                    e_rest(2)
                if more:
                    x_rest(2 * p + 2)
                if p == 0:
                    w_rest(2, w2t, 0)
                block_rest(1, p, 0)
                if more:
                    e_build(2 * p + 3, 0)
                block_rest(1, p, 1)
                third_rows(b2_st, ("b2", p), SCALE2)
                if p == 0:
                    w_rest(2, w2t, 1)
                block_rest(1, p, 2)
                third_rows(a3_st, ("a3", p), 1.0)
                if p == 0:
                    w_rest(2, w2t, 2)
                if more:
                    e_build(2 * p + 3, 1)
                block_rest(1, p, 3)
                b3_rest(p)
                if p == 0:
                    w_rest(2, w2t, 3)
                if more:
                    e_rest(2 * p + 3)
                    x1_take(2 * p + 2)
                low_take(2, p)
                block_rest(2, p, 0)
                if more:
                    x1_rest(2 * p + 2)
                if 2 * p + 4 < B:
                    e_build(2 * p + 4, 0)
                block_rest(2, p, 1)
                if more:
                    x_rest(2 * p + 3)
                block_rest(2, p, 2)
                if 2 * p + 4 < B:
                    e_build(2 * p + 4, 1)
                block_rest(2, p, 3)
                if 2 * p + 4 < B:
                    e_rest(2 * p + 4)
                if more:
                    x1_take(2 * p + 3)
                low_take(3, p)
                if more:
                    x1_rest(2 * p + 3)


_INS = ["x", "condB_coeff", "itok_B_0_2", "itok_B_14_62", "itok_B_3_7", "mask_Bx4096x4096_ik1",
        "L0_cond_W", "L0_cond_b", "L1_cond_W", "L1_cond_lora_A", "L1_cond_lora_B_w",
        "L2_cond_W", "L2_cond_b", "L2_cond_lora_A", "L2_cond_lora_B", "L3_cond_A", "L3_cond_B"]


def kernel(**inputs):
    import numpy as _np
    import concourse.bacc as _bacc
    from concourse import mybir as _mybir
    from concourse.bass_utils import run_bass_kernel_spmd as _run

    nc = _bacc.Bacc("TRN2", target_bir_lowering=False, num_devices=1)
    arrays, args = {}, []
    for name in _INS:
        a = _np.ascontiguousarray(inputs[name])
        arrays[f"in_{name}_dram"] = a
        args.append(nc.dram_tensor(f"in_{name}_dram", a.shape, _mybir.dt.from_np(a.dtype), kind="ExternalInput").ap())
    rows, half = _np.arange(128) // 16 % 2, _np.arange(256) // 128
    consts = _np.concatenate([_np.eye(128, dtype=_np.float32),
                              (rows[:, None] == half[None, :]).astype(_np.float32)], axis=1)
    arrays["consts_dram"] = _np.ascontiguousarray(consts)
    args.append(nc.dram_tensor("consts_dram", consts.shape, _mybir.dt.float32, kind="ExternalInput").ap())
    args.append(nc.dram_tensor("out_dram", (8, 128, 512), _mybir.dt.float32, kind="ExternalOutput").ap())
    lora_stack_kernel(nc, *args)
    r = _run(nc, [arrays], core_ids=[0])
    return r.results[0]["out_dram"]
```

```python
from contextlib import ExitStack

import concourse.bass as bass
from concourse import mybir

P = 128
F32 = mybir.dt.float32
F32R = mybir.dt.float32r
I32 = mybir.dt.int32
ALU = mybir.AluOpType
ACT = mybir.ActivationFunctionType


def lora_stack_kernel(nc, x, coeff, idx1, idx2, idx3, mask, w0, b0, w1, a1, b1, w2, b2, a2, bm2, a3, bm3, consts, out):
    B, S, D = x.shape
    C = D // P
    NPAIR = B // 2
    R1 = a1.shape[2]
    R2 = a2.shape[2]
    R3 = bm3.shape[2]
    Q = 4
    SCALE1, SCALE2 = 0.5, 2.0
    W2B = 2 * S
    assert S == P and R1 * Q == P and 2 * R2 * Q == P and 2 * R3 * Q == P

    groups = [("x", 0), ("x", 1), ("x1", 0), ("x1", 1)]
    for p in range(NPAIR - 1):
        groups += [("x", 2 * p + 2), ("x1", 2 * p + 2), ("x", 2 * p + 3), ("x1", 2 * p + 3)]
    number = {g: n for n, g in enumerate(groups)}
    low_number = {(layer, p): 3 * p + layer - 1 for p in range(NPAIR) for layer in (1, 2, 3)}

    raws = [("m", 0), ("m", 1), ("w", 1), ("m", 2), ("w", 2)] + [("m", b) for b in range(3, B)]
    RAW = 4
    POOL_BLOCKS = {1: 3, 2: 2}
    raw_number = {g: n for n, g in enumerate(raws)}

    FIRST_HALF, SECOND_HALF = slice(0, C // 2), slice(C // 2, C)
    SINGLE = [slice(c, c + 1) for c in range(C)]

    with ExitStack() as ctx:
        def sb(name, shape, dt=F32):
            return ctx.enter_context(nc.sbuf_tensor(name, shape, dt))

        def ps(name, shape):
            return ctx.enter_context(nc.psum_tensor(name, shape, F32))

        def sem(name):
            return ctx.enter_context(nc.semaphore(name))

        ident = sb("ident", [P, P])[:, :]
        pairmask = sb("pairmask", [P, W2B])[:, :]
        idx_sb = sb("idx_sb", [1, 3 * B], I32)
        coeff_sb = sb("coeff_sb", [P, B])
        coeff2 = sb("coeff2", [P, B])
        ncoeff = sb("ncoeff", [P, B])
        xsum = sb("xsum", [P, B])
        b0_sb = sb("b0_sb", [P, D])
        b2_sb = sb("b2_sb", [P, C])
        junk = sb("junk", [P, D], mybir.dt.bfloat16)
        raw = [sb(f"raw{i}", [P, C, D]) for i in range(RAW)]
        x_in = [sb(f"x_in{i}", [P, 2, D]) for i in range(2)]
        a1_in = sb("a1_in", [P, C, 4, R1])
        a2_in = sb("a2_in", [P, C, 4, R2])
        b3_in = sb("b3_in", [P, C, 4, R3])
        b1_in = sb("b1_in", [P, D])
        rows_in = sb("rows_in", [P, 2, 2, D])
        w0t = sb("w0t", [P, C, D])
        w1t = [sb(f"w1t_{s}", [P, C, D], F32R) for s in ("hi", "lo")]
        w2t = [sb(f"w2t_{s}", [P, C, D], F32R) for s in ("hi", "lo")]
        e_hi_sb = [sb(f"e_hi{i}", [P, C, D], F32R) for i in range(2)]
        e_sum_sb = [sb(f"e_sum{i}", [P, C, D]) for i in range(2)]
        e_lo_sb = [sb(f"e_lo{i}", [P, C, D], F32R) for i in range(2)]
        xt = [[sb(f"xt{i}_{s}", [P, C, S], F32R) for s in ("hi", "lo")] for i in range(2)]
        x1_sb = [sb(f"x1_{i}", [P, D]) for i in range(2)]
        x1t = [sb(f"x1t_{s}", [P, C, W2B], F32R) for s in ("hi", "lo")]
        x2t = [sb(f"x2t_{s}", [P, C, W2B], F32R) for s in ("hi", "lo")]
        x3t_whole = sb("x3t_whole", [P, C, W2B])
        x3t = [sb(f"x3t_{s}", [P, C, W2B], F32R) for s in ("hi", "lo")]
        a1_st = sb("a1_st", [P, C, 2, Q, R1], F32R)
        a2_st = sb("a2_st", [P, C, Q, 2 * R2], F32R)
        b3_st = sb("b3_st", [P, C, Q, 2 * R3], F32R)
        b1_st = sb("b1_st", [P, D], F32R)
        b2_st = sb("b2_st", [P, D], F32R)
        a3_st = sb("a3_st", [P, D], F32R)
        low_sb = sb("low_sb", [P, W2B], F32R)
        out_sb = [sb(f"out_sb{i}", [P, D]) for i in range(2)]

        ps_a = [ps(f"ps_a{i}", [P, D]) for i in range(2)]
        ps_t = [ps(f"ps_t{i}", [P, C, P]) for i in range(2)]
        ps_l = [ps(f"ps_l{i}", [P, D])[:, 0:W2B] for i in range(2)]
        ps_low = ps("ps_low", [P, D])
        ps_o = ps("ps_o", [P, D])

        ident_in = sem("ident_in")
        pairmask_in = sem("pairmask_in")
        coeff_in = sem("coeff_in")
        bias_in = sem("bias_in")
        idx_in = sem("idx_in")
        w0_in = [sem(f"w0_in{h}") for h in range(2)]
        raw_in = [[sem(f"raw{i}_in{h}") for h in range(2)] for i in range(RAW)]
        x_arrived = [sem(f"x_arrived{i}") for i in range(2)]
        b1_rows_in = sem("b1_rows_in")
        rows_spread = [sem(f"rows_spread{p}") for p in range(NPAIR)]
        picked_a1 = [sem(f"picked_a1_{p}") for p in range(NPAIR)]
        picked = [sem(f"picked{p}") for p in range(NPAIR)]
        w0_ready = sem("w0_ready")
        diag_added = {k: sem(f"diag{k}_added") for k in (1, 2)}
        w_hi = {k: sem(f"w{k}_hi") for k in (1, 2)}
        w_lo = {k: [sem(f"w{k}_lo_pool"), sem(f"w{k}_lo_dve")] for k in (1, 2)}
        x3_kept = sem("x3_kept")
        coeff_ready = sem("coeff_ready")
        row_hi = {g: sem(f"{g}_rows_hi") for g in ("b1", "b2", "a3")}
        row_done = {g: sem(f"{g}_rows_done") for g in ("b1", "b2", "a3")}
        a1_hi = sem("a1_hi")
        a2_hi = sem("a2_hi")
        b3_hi = sem("b3_hi")
        a1_done = sem("a1_done")
        a2_done = sem("a2_done")
        b3_done = sem("b3_done")
        xsum_done = sem("xsum_done")
        tr_ready = sem("tr_ready")
        tr_hi = sem("tr_hi")
        tr_done = sem("tr_done")
        e_sum = sem("e_sum")
        e_hi = sem("e_hi")
        e_lo = [sem(f"e_lo_half{h}") for h in range(2)]
        a_ready = sem("a_ready")
        x1_done = sem("x1_done")
        low_ready = sem("low_ready")
        low_hi = sem("low_hi")
        low_done = sem("low_done")
        l_ready = sem("l_ready")
        l_hi = sem("l_hi")
        l_done = sem("l_done")
        o_ready = sem("o_ready")
        o_done = [sem(f"o_done{i}") for i in range(2)]
        out_sent = [sem(f"out_sent{i}") for i in range(2)]

        block = ctx.enter_context(nc.Block())

        @block.sync
        def _(sp):
            def load_half(dst, src, h, arrived):
                part = slice(2 * h, 2 * h + 2)
                sp.dma_start(dst[:, part, :], src.rearrange("(c p) n -> p c n", p=P)[:, part, :]).then_inc(arrived, 16)

            def load_raw(kind, n, halves=(0, 1)):
                i = raw_number[kind, n]
                if i >= RAW:
                    was, m = raws[i - RAW]
                    if was == "m":
                        sp.wait_ge(e_sum, C * m + C)
                    else:
                        sp.wait_ge(w_lo[m][0], POOL_BLOCKS[m])
                        sp.wait_ge(w_lo[m][1], C - POOL_BLOCKS[m])
                if kind == "w":
                    src, dst = {1: w1, 2: w2}[n], raw[i % RAW][:, :, :]
                else:
                    src, dst = mask[n], raw[i % RAW][:, :, :].bitcast(I32)
                for h in halves:
                    load_half(dst, src, h, raw_in[i % RAW][h])

            def load_x(p):
                if p >= 2:
                    sp.wait_ge(tr_ready, number["x", 2 * p - 3] + 1)
                    sp.wait_ge(xsum_done, 2 * p - 2)
                sp.dma_start(x_in[p % 2][:, :, :],
                             x[2 * p:2 * p + 2].rearrange("b s d -> s b d")).then_inc(x_arrived[p % 2], 16)

            def index(k, b, n):
                return sp.value_load(idx_sb[0:1, k * B + b:k * B + b + 1], min_val=0, max_val=n - 1)

            def pick_a1(p):
                if p >= 2:
                    sp.wait_ge(a1_done, 2 * p - 2)
                for b in (2 * p, 2 * p + 1):
                    i1 = index(0, b, a1.shape[0])
                    sp.dma_start(a1_in[:, :, b % 4, :],
                                 a1[bass.ds(i1, 1)].rearrange("l (c p) r -> p (l c) r", p=P)).then_inc(picked_a1[p], 16)

            def pick(p):
                if p >= 2:
                    sp.wait_ge(a2_done, p - 1)
                    sp.wait_ge(b3_done, p - 1)
                    sp.wait_ge(row_done["b2"], p - 1)
                    sp.wait_ge(row_done["a3"], p - 1)
                for b in (2 * p, 2 * p + 1):
                    i2 = index(1, b, a2.shape[0])
                    sp.dma_start(a2_in[:, :, b % 4, :],
                                 a2[bass.ds(i2, 1)].rearrange("l (c p) r -> p (l c) r", p=P)).then_inc(picked[p], 16)
                    sp.dma_start(rows_in[R2 * (b % 2):R2 * (b % 2) + R2, p % 2, 0, :],
                                 bm2[bass.ds(i2, 1)].rearrange("l r o -> (l r) o")).then_inc(picked[p], 16)
                    i3 = index(2, b, a3.shape[0])
                    sp.dma_start(rows_in[R3 * (b % 2):R3 * (b % 2) + R3, p % 2, 1, :],
                                 a3[bass.ds(i3, 1)].rearrange("l r o -> (l r) o")).then_inc(picked[p], 16)
                    sp.dma_start(b3_in[:, :, b % 4, :],
                                 bm3[bass.ds(i3, 1)].rearrange("l (c p) r -> p (l c) r", p=P)).then_inc(picked[p], 16)

            def spread(p):
                sp.wait_ge(picked[p], 16 * 8)
                for g in range(1, Q):
                    sp.dma_start(rows_in[g * R1:(g + 1) * R1, p % 2, :, :], rows_in[0:R1, p % 2, :, :])\
                      .then_inc(rows_spread[p], 16)

            sp.dma_start(ident, consts[:, 0:P]).then_inc(ident_in, 16)
            for h in range(2):
                load_half(w0t, w0, h, w0_in[h])
                load_raw("m", 0, (h,))
                if h == 0:
                    load_x(0)
            for k, src in enumerate((idx1, idx2, idx3)):
                sp.dma_start(idx_sb[0:1, k * B:(k + 1) * B], src.rearrange("(a n) -> a n", a=1)).then_inc(idx_in, 16)
            load_raw("m", 1)
            load_raw("w", 1)
            sp.wait_ge(idx_in, 48)
            pick_a1(0)
            for g in range(Q):
                sp.dma_start(b1_in[g * R1:(g + 1) * R1, :], b1).then_inc(b1_rows_in, 16)
            load_x(1)
            load_raw("m", 2)
            load_raw("w", 2)
            pick(0)
            load_raw("m", 3)
            spread(0)
            for p in range(NPAIR):
                if p + 1 < NPAIR:
                    pick_a1(p + 1)
                if p + 2 < NPAIR:
                    load_x(p + 2)
                    load_raw("m", 2 * p + 4)
                    load_raw("m", 2 * p + 5)
                if p + 1 < NPAIR:
                    pick(p + 1)
                    spread(p + 1)
                for b in (2 * p, 2 * p + 1):
                    sp.wait_ge(o_done[b % 2], p + 1)
                    sp.dma_start(out[b], out_sb[b % 2][:, :]).then_inc(out_sent[b % 2], 16)
            for i in range(2):
                sp.wait_ge(out_sent[i], 16 * NPAIR)

        @block.gpsimd
        def _(pool):
            def w_rest(k, w):
                for c in range(POOL_BLOCKS[k]):
                    pool.wait_ge(w_hi[k], c + 1)
                    nc.gpsimd.tensor_tensor(w[1][:, c, :], raw[raw_number["w", k] % RAW][:, c, :],
                                            w[0][:, c, :].bitcast(F32), ALU.subtract).then_inc(w_lo[k][0], 1)

            def e_rest(b, blocks=(SECOND_HALF,)):
                for part in blocks:
                    pool.wait_ge(e_hi, C * b + part.stop)
                    nc.gpsimd.tensor_tensor(e_lo_sb[b % 2][:, part, :], e_sum_sb[b % 2][:, part, :],
                                            e_hi_sb[b % 2][:, part, :].bitcast(F32), ALU.subtract)\
                             .then_inc(e_lo[1], part.stop - part.start)

            def diagonal(k):
                i = raw_number["w", k]
                for c in range(C):
                    if c % 2 == 0:
                        pool.wait_ge(raw_in[i % RAW][c // 2], 16 * (i // RAW + 1))
                    d = raw[i % RAW][:, c, c * P:(c + 1) * P]
                    nc.gpsimd.tensor_tensor(d, d, ident, ALU.add).then_inc(diag_added[k], 1)

            def w0_diagonal(h):
                pool.wait_ge(w0_in[h], 16)
                for c in (2 * h, 2 * h + 1):
                    d = w0t[:, c, c * P:(c + 1) * P]
                    nc.gpsimd.tensor_tensor(d, d, ident, ALU.add).then_inc(w0_ready, 1)

            pool.dma_start(coeff_sb[:, :], coeff.partition_broadcast(P)).then_inc(coeff_in, 16)
            pool.wait_ge(ident_in, 16)
            w0_diagonal(0)
            pool.wait_ge(raw_in[raw_number["m", 0]][0], 16)
            pool.dma_start(pairmask, consts[:, P:P + W2B]).then_inc(pairmask_in, 16)
            pool.dma_start(b0_sb[:, :], b0.partition_broadcast(P)).then_inc(bias_in, 16)
            pool.dma_start(b2_sb[:, :], b2.rearrange("(c p) -> p c", p=P),
                           allow_slow_non_contiguous=True).then_inc(bias_in, 16)
            w0_diagonal(1)
            e_rest(0, SINGLE[C // 2:])
            diagonal(1)
            w_rest(1, w1t)
            e_rest(2)
            w_rest(2, w2t)
            for b in range(4, B):
                e_rest(b)

        @block.tensor
        def _(pe):
            def group(g, src):
                n = number[g]
                if n >= 2:
                    pe.wait_ge(tr_done, n - 1)
                for c in range(C):
                    last = pe.transpose(ps_t[n % 2][:, c, :], src[:, c * P:(c + 1) * P], ident)
                last.then_inc(tr_ready, 1)

            def x_turn(b):
                pe.wait_ge(x_arrived[b // 2 % 2], 16 * (b // 4 + 1))
                group(("x", b), x_in[b // 2 % 2][:, b % 2, :])

            def x1_turn(b):
                pe.wait_ge(x1_done, b + 1)
                group(("x1", b), x1_sb[b % 2])

            def keep_busy(n):
                for _ in range(n):
                    pe.matmul(ps_o[:, 0:P], ident, ident, is_transpose=True, start=True, stop=True)

            def natural(b, halfway=None):
                pe.wait_ge(tr_done, number["x", b] + 1)
                if b >= 2:
                    pe.wait_ge(x1_done, b - 1)
                if b % 2 == 0 and b >= 4:
                    pe.wait_ge(o_done[1], b // 2 - 1)
                xh, xl = xt[b % 2]
                eh, el = e_hi_sb[b % 2], e_lo_sb[b % 2]
                for c in range(C):
                    if c == C // 2 and halfway:
                        halfway()
                    pe.wait_ge(e_hi, C * b + c + 1)
                    pe.matmul(ps_a[b % 2][:, :], xh[:, c, :], eh[:, c, :], start=(c == 0), stop=False)
                    pe.matmul(ps_a[b % 2][:, :], xl[:, c, :], eh[:, c, :], start=False, stop=False)
                for c in range(C):
                    pe.wait_ge(e_lo[c // 2], 2 * b + c % 2 + 1)
                    last = pe.matmul(ps_a[b % 2][:, :], xh[:, c, :], el[:, c, :], start=False, stop=(c == C - 1))
                last.then_inc(a_ready, 1)

            def low(layer, p, src, stack):
                n = low_number[layer, p]
                if n:
                    pe.wait_ge(low_done, n)
                if layer == 1:
                    for b in range(2):
                        if b == 1:
                            pe.wait_ge(tr_done, number["x1", 2 * p + 1] + 1)
                        for c in range(C):
                            for s in range(2):
                                last = pe.matmul(ps_low[:, b * S:(b + 1) * S], stack[:, c, b, :, :],
                                                 src[s][:, c, b * S:b * S + S],
                                                 start=(c == 0 and s == 0), stop=(c == C - 1 and s == 1))
                else:
                    for c in range(C):
                        pe.wait_ge(l_done, 8 * p + 4 * (layer - 2) + c + 1)
                        for s in range(2):
                            last = pe.matmul(ps_low[:, 0:W2B], stack[:, c, :, :], src[s][:, c, :],
                                             start=(c == 0 and s == 0), stop=(c == C - 1 and s == 1))
                last.then_inc(low_ready, 1)

            def turned(layer, p, src, w, second, fill):
                for o in range(C):
                    if (layer == 1) == (o >= 2):
                        pe.wait_ge(l_done, 8 * p + o - 1 + 4 * (layer - 1))
                    elif p or layer == 2:
                        pe.wait_ge(x3_kept, C * p + o - 1)
                    cols = slice(o * P, (o + 1) * P)
                    for c in range(C):
                        if p == 0 and o == 0:
                            if c < POOL_BLOCKS[layer]:
                                pe.wait_ge(w_lo[layer][0], c + 1)
                            else:
                                pe.wait_ge(w_lo[layer][1], c + 1 - POOL_BLOCKS[layer])
                        pe.matmul(ps_l[o % 2], w[0][:, c, cols], src[0][:, c, :], start=(c == 0), stop=False)
                        pe.matmul(ps_l[o % 2], w[0][:, c, cols], src[1][:, c, :], start=False, stop=False)
                        pe.matmul(ps_l[o % 2], w[1][:, c, cols], src[0][:, c, :], start=False, stop=False)
                    if o == 0:
                        pe.wait_ge(low_done, low_number[layer, p] + 1)
                        if layer == 1:
                            pe.wait_ge(row_done["b1"], 1)
                        else:
                            pe.wait_ge(row_done["b2"], p + 1)
                    pe.matmul(ps_l[o % 2], second[:, cols], low_sb[:, :], start=False, stop=True)\
                        .then_inc(l_ready, 1)
                    fill(o)

            def layer1(p):
                def fill(o):
                    if o == 0 and p + 1 < NPAIR:
                        x_turn(2 * p + 2)

                pe.wait_ge(tr_done, number["x1", 2 * p] + 1)
                pe.wait_ge(a1_done, 2 * p + 2)
                low(1, p, x1t, a1_st)
                turned(1, p, x1t, w1t, b1_st, fill)

            def layer2(p):
                def fill(o):
                    if o == 0 and p + 1 < NPAIR:
                        x1_turn(2 * p + 2)
                    if o == 1 and p + 1 < NPAIR:
                        x_turn(2 * p + 3)

                pe.wait_ge(a2_done, p + 1)
                low(2, p, x2t, a2_st)
                turned(2, p, x2t, w2t, b2_st, fill)

            def layer3(p):
                banks = (ps_o, ps_a[0])

                def to_rows():
                    for c in range(C):
                        pe.wait_ge(x3_kept, C * p + c + 1)
                        for b in range(2):
                            pe.matmul(banks[b][:, c * P:(c + 1) * P], x3t_whole[:, c, b * S:(b + 1) * S], ident,
                                      is_transpose=True, start=(c == 0), stop=False, skip_group_check=True)

                if p:
                    for done in o_done:
                        pe.wait_ge(done, p)
                pe.wait_ge(x1_done, min(2 * p + 3, B))
                pe.wait_ge(b3_done, p + 1)
                if p + 1 < NPAIR:
                    low(3, p, x3t, b3_st)
                    to_rows()
                    x1_turn(2 * p + 3)
                else:
                    to_rows()
                    low(3, p, x3t, b3_st)
                pe.wait_ge(low_done, low_number[3, p] + 1)
                pe.wait_ge(row_done["a3"], p + 1)
                for b in range(2):
                    pe.matmul(banks[b][:, :], low_sb[:, b * S:(b + 1) * S], a3_st[:, :], start=False, stop=True,
                              skip_group_check=True).then_inc(o_ready, 1)

            pe.wait_ge(ident_in, 16)
            keep_busy(20)
            x_turn(0)
            x_turn(1)
            keep_busy(8)
            natural(0, lambda: keep_busy(10))
            natural(1)
            x1_turn(0)
            x1_turn(1)
            for p in range(NPAIR):
                layer1(p)
                if p + 1 < NPAIR:
                    natural(2 * p + 2)
                layer2(p)
                if p + 1 < NPAIR:
                    natural(2 * p + 3)
                layer3(p)

        @block.scalar
        def _(act):
            def round_group(g, dst):
                act.wait_ge(tr_ready, number[g] + 1)
                act.activation(dst, ps_t[number[g] % 2][:, :, :], ACT.Copy).then_inc(tr_hi, 1)

            def x_sum(b):
                act.wait_ge(x_arrived[b // 2 % 2], 16 * (b // 4 + 1))
                act.wait_ge(coeff_ready, 2)
                if b:
                    act.wait_ge(xsum_done, b)
                act.activation(junk[:, :], x_in[b // 2 % 2][:, b % 2, :], ACT.Copy, scale=ncoeff[:, b:b + 1],
                               accum_out=xsum[:, b:b + 1]).then_inc(xsum_done, 1)

            def x_round(b):
                if b >= 2:
                    act.wait_ge(a_ready, b - 1)
                round_group(("x", b), xt[b % 2][0][:, :, :])

            def e_round(b, part):
                act.wait_ge(e_sum, C * b + part.stop)
                if b >= 2:
                    act.wait_ge(a_ready, b - 1)
                act.activation(e_hi_sb[b % 2][:, part, :], e_sum_sb[b % 2][:, part, :], ACT.Copy)\
                   .then_inc(e_hi, part.stop - part.start)

            def x1_round(b):
                round_group(("x1", b), x1t[0][:, :, (b % 2) * S:(b % 2 + 1) * S])

            def rows_round(g, p, dst, src, scale):
                if p:
                    act.wait_ge(*{"b2": (l_ready, 8 * p), "a3": (o_ready, 2 * p)}[g])
                act.activation(dst[:, :], src, ACT.Copy, scale=scale).then_inc(row_hi[g], 1)

            def block_round(layer, p, o):
                act.wait_ge(l_ready, 8 * p + 4 * (layer - 1) + o + 1)
                if layer == 1:
                    act.activation(x2t[0][:, o, :], ps_l[o % 2], ACT.Copy).then_inc(l_hi, 1)
                else:
                    if p and o == 0:
                        act.wait_ge(o_ready, 2 * p)
                    act.activation(x3t_whole[:, o, :], ps_l[o % 2], ACT.Identity, bias=b2_sb[:, o:o + 1])\
                       .then_inc(x3_kept, 1)
                    act.wait_ge(x3_kept, C * p + o + 1)
                    act.activation(x3t[0][:, o, :], x3t_whole[:, o, :], ACT.Copy).then_inc(l_hi, 1)

            def outs(p):
                for b in range(2 if p + 1 < NPAIR else 1):
                    act.wait_ge(o_ready, 2 * p + b + 1)
                    if p:
                        act.wait_ge(out_sent[b], 16 * p)
                    act.activation(out_sb[b][:, :], (ps_o, ps_a[0])[b][:, :], ACT.Copy).then_inc(o_done[b], 1)

            def pair_of(t, p):
                return t[:, :, p % 2 * 2:p % 2 * 2 + 2, :].rearrange("p c b r -> p c (b r)")

            def b2_round(p):
                act.wait_ge(rows_spread[p], 16 * 3)
                rows_round("b2", p, b2_st, rows_in[:, p % 2, 0, :], SCALE2)

            def a3_round(p):
                act.wait_ge(rows_spread[p], 16 * 3)
                rows_round("a3", p, a3_st, rows_in[:, p % 2, 1, :], 1.0)

            def a1_stack(p):
                act.wait_ge(picked_a1[p], 16 * 2)
                if p:
                    act.wait_ge(low_ready, low_number[1, p - 1] + 1)
                for b in range(2):
                    act.activation(a1_st[:, :, b, 0:Q - 1, :],
                                   a1_in[:, :, p % 2 * 2 + b, :].unsqueeze(2).broadcast_to([P, C, Q - 1, R1]),
                                   ACT.Copy).then_inc(a1_hi, 1)

            def a2_stack(p):
                act.wait_ge(picked[p], 16 * 8)
                if p:
                    act.wait_ge(low_ready, low_number[2, p - 1] + 1)
                act.activation(a2_st[:, :, 0:Q - 1, :],
                               pair_of(a2_in, p).unsqueeze(2).broadcast_to([P, C, Q - 1, 2 * R2]),
                               ACT.Copy).then_inc(a2_hi, 1)

            def b3_stack(p):
                act.wait_ge(picked[p], 16 * 8)
                if p:
                    act.wait_ge(low_ready, low_number[3, p - 1] + 1)
                act.activation(b3_st[:, :, 0:Q - 1, :],
                               pair_of(b3_in, p).unsqueeze(2).broadcast_to([P, C, Q - 1, 2 * R3]),
                               ACT.Copy).then_inc(b3_hi, 1)

            def w_round(k, w, blocks):
                for c in blocks:
                    act.wait_ge(diag_added[k], c + 1)
                    act.activation(w[0][:, c, :], raw[raw_number["w", k] % RAW][:, c, :], ACT.Copy)\
                       .then_inc(w_hi[k], 1)

            act.wait_ge(coeff_in, 16)
            act.activation(ncoeff[:, :], coeff_sb[:, :], ACT.Copy, scale=-1.0).then_inc(coeff_ready, 1)
            e_round(0, FIRST_HALF)
            x_round(0)
            x_round(1)
            e_round(0, SINGLE[2])
            e_round(0, SINGLE[3])
            x_sum(0)
            e_round(1, FIRST_HALF)
            e_round(1, SINGLE[2])
            e_round(1, SINGLE[3])
            x_sum(1)
            w_round(1, w1t, (0, 1))
            a1_stack(0)
            x1_round(0)
            x1_round(1)
            w_round(1, w1t, (2, 3))
            act.wait_ge(b1_rows_in, 16 * Q)
            rows_round("b1", 0, b1_st, b1_in[:, :], SCALE1)
            act.wait_ge(bias_in, 32)

            block_round(1, 0, 0)
            x_round(2)
            e_round(2, FIRST_HALF)
            block_round(1, 0, 1)
            e_round(2, SECOND_HALF)
            w_round(2, w2t, (0,))
            block_round(1, 0, 2)
            w_round(2, w2t, (1, 2))
            block_round(1, 0, 3)
            w_round(2, w2t, (3,))
            a2_stack(0)
            x_sum(2)
            b2_round(0)
            block_round(2, 0, 0)
            e_round(3, FIRST_HALF)
            x1_round(2)
            block_round(2, 0, 1)
            x_round(3)
            block_round(2, 0, 2)
            e_round(3, SECOND_HALF)
            block_round(2, 0, 3)
            b3_stack(0)
            a3_round(0)
            a1_stack(1)
            x_sum(3)
            x1_round(3)
            a2_stack(1)
            b2_round(1)
            outs(0)
            e_round(4, FIRST_HALF)

            for p in range(1, NPAIR):
                more = p + 1 < NPAIR
                block_round(1, p, 0)
                if p == 1:
                    e_round(4, SECOND_HALF)
                if more:
                    x_round(2 * p + 2)
                block_round(1, p, 1)
                b3_stack(p)
                if more:
                    x_sum(2 * p + 2)
                block_round(1, p, 2)
                if more:
                    e_round(2 * p + 3, FIRST_HALF)
                a3_round(p)
                block_round(1, p, 3)
                if more:
                    e_round(2 * p + 3, SECOND_HALF)
                    a1_stack(p + 1)
                block_round(2, p, 0)
                if more:
                    x1_round(2 * p + 2)
                block_round(2, p, 1)
                if more:
                    x_round(2 * p + 3)
                if 2 * p + 4 < B:
                    e_round(2 * p + 4, FIRST_HALF)
                block_round(2, p, 2)
                block_round(2, p, 3)
                if more:
                    x_sum(2 * p + 3)
                if 2 * p + 4 < B:
                    e_round(2 * p + 4, SECOND_HALF)
                if more:
                    a2_stack(p + 1)
                    b2_round(p + 1)
                    x1_round(2 * p + 3)
                outs(p)

        @block.vector
        def _(dve):
            def rest_group(g, dst, hi):
                dve.wait_ge(tr_hi, number[g] + 1)
                dve.tensor_tensor(dst, ps_t[number[g] % 2][:, :, :], hi.bitcast(F32), ALU.subtract)\
                   .then_inc(tr_done, 1)

            def x_rest(b):
                rest_group(("x", b), xt[b % 2][1][:, :, :], xt[b % 2][0][:, :, :])

            def e_build(b, part):
                i = raw_number["m", b]
                h = part.start // 2
                dve.wait_ge(raw_in[i % RAW][h], 16 * (i // RAW + 1))
                if b == 0:
                    dve.wait_ge(w0_ready, part.stop)
                if b >= 2:
                    dve.wait_ge(e_lo[h], 2 * (b - 1))
                dve.scalar_tensor_tensor(e_sum_sb[b % 2][:, part, :], raw[i % RAW][:, part, :].bitcast(I32),
                                         coeff2[:, b:b + 1], w0t[:, part, :], ALU.mult, ALU.add)\
                   .then_inc(e_sum, part.stop - part.start)

            def e_rest(b, part=FIRST_HALF):
                h = part.start // 2
                dve.wait_ge(e_hi, C * b + part.stop)
                if h:
                    dve.wait_ge(e_lo[1], 2 * b)
                dve.tensor_tensor(e_lo_sb[b % 2][:, part, :], e_sum_sb[b % 2][:, part, :],
                                  e_hi_sb[b % 2][:, part, :].bitcast(F32), ALU.subtract)\
                   .then_inc(e_lo[h], part.stop - part.start)

            def x1_take(b):
                dve.wait_ge(a_ready, b + 1)
                dve.wait_ge(xsum_done, b + 1)
                if b >= 2:
                    dve.wait_ge(tr_ready, number["x1", b - 2] + 1)
                dve.scalar_tensor_tensor(x1_sb[b % 2][:, :], ps_a[b % 2][:, :], xsum[:, b:b + 1], b0_sb[:, :],
                                         ALU.add, ALU.add).then_inc(x1_done, 1)

            def x1_rest(b):
                cols = slice((b % 2) * S, (b % 2 + 1) * S)
                rest_group(("x1", b), x1t[1][:, :, cols], x1t[0][:, :, cols])

            def third_rows(g, p, t, src, scale):
                dve.wait_ge(row_hi[g], p + 1)
                part = t[2 * R1:3 * R1, :]
                dve.scalar_tensor_tensor(part, src[2 * R1:3 * R1], scale, part.bitcast(F32), ALU.mult, ALU.subtract)\
                   .then_inc(row_done[g], 1)

            def low_take(layer, p):
                n = low_number[layer, p]
                dve.wait_ge(low_ready, n + 1)
                rows = slice(R1, 2 * R1)
                if layer == 1:
                    dve.tensor_copy(low_sb[:, :], ps_low[:, 0:W2B]).then_inc(low_hi, 1)
                    dve.wait_ge(low_hi, n + 1)
                    dve.tensor_tensor(low_sb[rows, :], ps_low[rows, 0:W2B], low_sb[rows, :].bitcast(F32),
                                      ALU.subtract).then_inc(low_done, 1)
                    return
                if n == 1:
                    dve.wait_ge(pairmask_in, 16)
                dve.tensor_tensor(low_sb[:, :], ps_low[:, 0:W2B], pairmask, ALU.mult).then_inc(low_hi, 1)
                dve.wait_ge(low_hi, n + 1)
                for b in range(2):
                    cols = slice(b * S, (b + 1) * S)
                    last = dve.scalar_tensor_tensor(low_sb[rows, cols], ps_low[rows, cols],
                                                    pairmask[rows, b * S:b * S + 1], low_sb[rows, cols].bitcast(F32),
                                                    ALU.mult, ALU.subtract)
                last.then_inc(low_done, 1)

            def block_rest(layer, p, o):
                dve.wait_ge(l_hi, 8 * p + 4 * (layer - 1) + o + 1)
                if layer == 1:
                    dve.tensor_tensor(x2t[1][:, o, :], ps_l[o % 2], x2t[0][:, o, :].bitcast(F32),
                                      ALU.subtract).then_inc(l_done, 1)
                else:
                    dve.tensor_tensor(x3t[1][:, o, :], x3t_whole[:, o, :], x3t[0][:, o, :].bitcast(F32),
                                      ALU.subtract).then_inc(l_done, 1)

            def w_rest(k, w):
                for c in range(POOL_BLOCKS[k], C):
                    dve.wait_ge(w_hi[k], c + 1)
                    dve.tensor_tensor(w[1][:, c, :], raw[raw_number["w", k] % RAW][:, c, :],
                                      w[0][:, c, :].bitcast(F32), ALU.subtract).then_inc(w_lo[k][1], 1)

            def diagonal(k):
                i = raw_number["w", k]
                for c in range(C):
                    if c % 2 == 0:
                        dve.wait_ge(raw_in[i % RAW][c // 2], 16 * (i // RAW + 1))
                    d = raw[i % RAW][:, c, c * P:(c + 1) * P]
                    dve.tensor_tensor(d, d, ident, ALU.add).then_inc(diag_added[k], 1)

            def a1_rest(p):
                for b in range(2):
                    dve.wait_ge(a1_hi, 2 * p + b + 1)
                    dve.tensor_tensor(a1_st[:, :, b, Q - 1, :], a1_in[:, :, p % 2 * 2 + b, :],
                                      a1_st[:, :, b, 0, :].bitcast(F32), ALU.subtract).then_inc(a1_done, 1)

            def a2_rest(p):
                dve.wait_ge(a2_hi, p + 1)
                src = a2_in[:, :, p % 2 * 2:p % 2 * 2 + 2, :].rearrange("p c b r -> p c (b r)")
                dve.tensor_tensor(a2_st[:, :, Q - 1, :], src, a2_st[:, :, 0, :].bitcast(F32),
                                  ALU.subtract).then_inc(a2_done, 1)

            def b3_rest(p):
                dve.wait_ge(b3_hi, p + 1)
                src = b3_in[:, :, p % 2 * 2:p % 2 * 2 + 2, :].rearrange("p c b r -> p c (b r)")
                dve.tensor_tensor(b3_st[:, :, Q - 1, :], src, b3_st[:, :, 0, :].bitcast(F32),
                                  ALU.subtract).then_inc(b3_done, 1)

            def b2_rest(p):
                third_rows("b2", p, b2_st, rows_in[:, p % 2, 0, :], SCALE2)

            def a3_rest(p):
                third_rows("a3", p, a3_st, rows_in[:, p % 2, 1, :], 1.0)

            dve.wait_ge(coeff_in, 16)
            dve.tensor_scalar(coeff2[:, :], coeff_sb[:, :], 2.0, None, ALU.mult).then_inc(coeff_ready, 1)
            dve.wait_ge(coeff_ready, 2)
            dve.wait_ge(ident_in, 16)
            e_build(0, FIRST_HALF)
            e_rest(0)
            x_rest(0)
            x_rest(1)
            e_build(0, SINGLE[2])
            e_build(0, SINGLE[3])
            e_build(1, FIRST_HALF)
            e_build(1, SINGLE[2])
            e_build(1, SINGLE[3])
            e_rest(1)
            e_rest(1, SECOND_HALF)
            dve.wait_ge(bias_in, 32)
            x1_take(0)
            x1_take(1)
            a1_rest(0)
            x1_rest(0)
            x1_rest(1)
            w_rest(1, w1t)
            third_rows("b1", 0, b1_st, b1_in, SCALE1)

            low_take(1, 0)
            e_build(2, FIRST_HALF)
            block_rest(1, 0, 0)
            x_rest(2)
            e_build(2, SECOND_HALF)
            block_rest(1, 0, 1)
            diagonal(2)
            block_rest(1, 0, 2)
            e_rest(2)
            block_rest(1, 0, 3)
            a2_rest(0)
            w_rest(2, w2t)
            x1_take(2)
            b2_rest(0)
            low_take(2, 0)
            e_build(3, FIRST_HALF)
            block_rest(2, 0, 0)
            e_build(3, SECOND_HALF)
            x1_rest(2)
            block_rest(2, 0, 1)
            x_rest(3)
            block_rest(2, 0, 2)
            e_rest(3)
            e_rest(3, SECOND_HALF)
            block_rest(2, 0, 3)
            b3_rest(0)
            a3_rest(0)
            x1_take(3)
            low_take(3, 0)
            a1_rest(1)
            x1_rest(3)
            a2_rest(1)
            e_build(4, FIRST_HALF)
            b2_rest(1)

            for p in range(1, NPAIR):
                more = p + 1 < NPAIR
                low_take(1, p)
                if p == 1:
                    e_build(4, SECOND_HALF)
                block_rest(1, p, 0)
                if more:
                    e_rest(2 * p + 2)
                    x_rest(2 * p + 2)
                block_rest(1, p, 1)
                if more:
                    e_build(2 * p + 3, FIRST_HALF)
                block_rest(1, p, 2)
                if more:
                    e_build(2 * p + 3, SECOND_HALF)
                block_rest(1, p, 3)
                if more:
                    x1_take(2 * p + 2)
                low_take(2, p)
                b3_rest(p)
                a3_rest(p)
                if more:
                    e_rest(2 * p + 3)
                block_rest(2, p, 0)
                if more:
                    x1_rest(2 * p + 2)
                if 2 * p + 4 < B:
                    e_build(2 * p + 4, FIRST_HALF)
                block_rest(2, p, 1)
                if more:
                    x_rest(2 * p + 3)
                    a1_rest(p + 1)
                block_rest(2, p, 2)
                if 2 * p + 4 < B:
                    e_build(2 * p + 4, SECOND_HALF)
                block_rest(2, p, 3)
                if more:
                    x1_take(2 * p + 3)
                low_take(3, p)
                if more:
                    a2_rest(p + 1)
                    x1_rest(2 * p + 3)
                    b2_rest(p + 1)

            dve.wait_ge(o_ready, B)
            dve.wait_ge(out_sent[1], 16 * (NPAIR - 1))
            dve.tensor_copy(out_sb[1][:, :], ps_a[0][:, :]).then_inc(o_done[1], 1)


_INS = ["x", "condB_coeff", "itok_B_0_2", "itok_B_14_62", "itok_B_3_7", "mask_Bx4096x4096_ik1",
        "L0_cond_W", "L0_cond_b", "L1_cond_W", "L1_cond_lora_A", "L1_cond_lora_B_w",
        "L2_cond_W", "L2_cond_b", "L2_cond_lora_A", "L2_cond_lora_B", "L3_cond_A", "L3_cond_B"]


def kernel(**inputs):
    import numpy as _np
    import concourse.bacc as _bacc
    from concourse import mybir as _mybir
    from concourse.bass_utils import run_bass_kernel_spmd as _run

    nc = _bacc.Bacc("TRN2", target_bir_lowering=False, num_devices=1)
    arrays, args = {}, []
    turned = {"L0_cond_W", "L1_cond_W", "L1_cond_lora_B_w", "L2_cond_W", "L2_cond_lora_B", "L3_cond_A", "L3_cond_B"}
    for name in _INS:
        a = _np.asarray(inputs[name])
        a = _np.ascontiguousarray(a.swapaxes(-1, -2) if name in turned else a)
        arrays[f"in_{name}_dram"] = a
        args.append(nc.dram_tensor(f"in_{name}_dram", a.shape, _mybir.dt.from_np(a.dtype), kind="ExternalInput").ap())
    rows, half = _np.arange(128) // 16 % 2, _np.arange(256) // 128
    consts = _np.concatenate([_np.eye(128, dtype=_np.float32),
                              (rows[:, None] == half[None, :]).astype(_np.float32)], axis=1)
    arrays["consts_dram"] = _np.ascontiguousarray(consts)
    args.append(nc.dram_tensor("consts_dram", consts.shape, _mybir.dt.float32, kind="ExternalInput").ap())
    args.append(nc.dram_tensor("out_dram", (8, 128, 512), _mybir.dt.float32, kind="ExternalOutput").ap())
    lora_stack_kernel(nc, *args)
    r = _run(nc, [arrays], core_ids=[0])
    return r.results[0]["out_dram"]
```
